# Optimizing a Trainium2 kernel written in Bass

```python
import numpy as np
import jax
import jax.numpy as jnp

def _softmax(x, axis=-1):
    return jax.nn.softmax(x, axis=axis)

def _gelu(x):
    return jax.nn.gelu(x, approximate=True)

def _silu(x):
    return jax.nn.silu(x)

def _sigmoid(x):
    return jax.nn.sigmoid(x)

def _layernorm(x, axis=-1, eps=1e-05):
    m = jnp.mean(x, axis=axis, keepdims=True)
    v = jnp.var(x, axis=axis, keepdims=True)
    return (x - m) / jnp.sqrt(v + eps)

def _scatter_add(tgt, idx, src, axis=0):
    return tgt.at[idx].add(src)

def _segment_sum(src, seg, n):
    return jax.ops.segment_sum(src, seg, n)
kernel_name = 'mk_hybrid_d2_jaxref_r8_54c0f6'

def setup_inputs(seed: int=0):
    np.random.seed(seed)
    _w = jnp.asarray

    def _L0_attn_a_setup():
        import jax, jax.numpy as jnp
        import numpy as np
        B, T, C = (2, 256, 128)
        H = 16
        D = C // H
        SCALE = 1.0 / np.sqrt(D)
        key = jax.random.key(seed)
        k1, k2, k3 = jax.random.split(key, 3)
        x = jax.random.normal(k1, (B, T, C), dtype=jnp.float32)
        Wqkv = jax.random.normal(k2, (C, 3 * C), dtype=jnp.float32) * 0.02
        bqkv = jnp.zeros((3 * C,), dtype=jnp.float32)
        Wo = jax.random.normal(k3, (C, C), dtype=jnp.float32) * 0.02
        bo = jnp.zeros((C,), dtype=jnp.float32)
        return {'x': x, 'Wqkv': Wqkv, 'bqkv': bqkv, 'Wo': Wo, 'bo': bo}
    _L0_attn_a_in = _L0_attn_a_setup()

    def _L0_attn_b_setup():
        import jax, jax.numpy as jnp
        import numpy as np
        B, T, C = (2, 256, 128)
        DIM, H = (128, 16)
        HD = DIM // H
        key = jax.random.key(seed)
        ks = jax.random.split(key, 6)
        s_in = 1.0 / np.sqrt(C)
        s_proj = 1.0 / np.sqrt(DIM)
        return {'x': jax.random.normal(ks[0], (B, T, C), dtype=jnp.float32), 'Wqkv': jax.random.normal(ks[1], (C, 3 * DIM), dtype=jnp.float32) * s_in, 'bqkv': jnp.zeros((3 * DIM,), dtype=jnp.float32), 'r_sigma': jnp.float32(0.1), 'Wproj': jax.random.normal(ks[2], (DIM, C), dtype=jnp.float32) * s_proj, 'bproj': jnp.zeros((C,), dtype=jnp.float32)}
    _L0_attn_b_in = _L0_attn_b_setup()

    def _L0_ffn_setup():
        import jax, jax.numpy as jnp
        import numpy as np
        NUM_OPS, B, T, D = (8, 8, 64, 128)
        key = jax.random.key(seed)
        k1, k2, k3, k4 = jax.random.split(key, 4)
        x = jax.random.normal(k1, (B, T, D), dtype=jnp.float32)
        W = jax.random.normal(k2, (NUM_OPS, D, D), dtype=jnp.float32) * 0.02
        b = jnp.zeros((NUM_OPS, D), dtype=jnp.float32)
        logits = 0.001 * jax.random.normal(k3, (NUM_OPS,), dtype=jnp.float32)
        u = jax.random.uniform(k4, (NUM_OPS,), dtype=jnp.float32, minval=1e-06, maxval=1.0 - 1e-06)
        return {'x': x, 'W': W, 'b': b, 'logits': logits, 'u': u}
    _L0_ffn_in = _L0_ffn_setup()

    def _L1_attn_a_setup():
        import jax, jax.numpy as jnp
        import numpy as np
        NUM_HEADS = 16

        def _sinusoid_rel_pos(seq_len, dim):
            pos = jnp.arange(seq_len - 1, -1, -1, dtype=jnp.float32)
            inv_freq = 1.0 / 10000.0 ** (jnp.arange(0, dim, 2, dtype=jnp.float32) / dim)
            ang = pos[:, None] * inv_freq[None, :]
            return jnp.concatenate([jnp.sin(ang), jnp.cos(ang)], axis=-1)

        def _rel_shift(x):
            B, H, S, L = x.shape
            x = jnp.pad(x, ((0, 0), (0, 0), (0, 0), (1, 0)))
            x = x.reshape(B, H, L + 1, S)
            return x[:, :, 1:S + 1, :]
        key = jax.random.key(seed)
        ks = jax.random.split(key, 8)
        B, S, C = (2, 256, 128)
        Dk, Dv, H = (128, 128, NUM_HEADS)
        dk = Dk // H
        scale = 0.02
        return {'x': jax.random.normal(ks[0], (B, S, C), dtype=jnp.float32), 'Wq': jax.random.normal(ks[1], (C, Dk), dtype=jnp.float32) * scale, 'Wk': jax.random.normal(ks[2], (C, Dk), dtype=jnp.float32) * scale, 'Wv': jax.random.normal(ks[3], (C, Dv), dtype=jnp.float32) * scale, 'u': jax.random.normal(ks[4], (H, dk), dtype=jnp.float32) * scale, 'v': jax.random.normal(ks[5], (H, dk), dtype=jnp.float32) * scale, 'Wo': jax.random.normal(ks[6], (Dv, C), dtype=jnp.float32) * scale, 'bo': jnp.zeros((C,), dtype=jnp.float32)}
    _L1_attn_a_in = _L1_attn_a_setup()

    def _L1_attn_b_setup():
        import jax, jax.numpy as jnp
        import numpy as np
        D_MODEL = 128
        NUM_HEADS = 16
        HEAD_DIM = D_MODEL // NUM_HEADS

        def _rope(x):
            B, H, T, d = x.shape
            pos = jnp.arange(T, dtype=x.dtype)[:, None]
            freq_seq = jnp.arange(d // 2, dtype=x.dtype)
            inv_freq = 1.0 / 10000.0 ** (freq_seq / (d // 2))
            ang = pos * inv_freq[None, :]
            sin = jnp.sin(ang)[None, None]
            cos = jnp.cos(ang)[None, None]
            x1, x2 = (x[..., :d // 2], x[..., d // 2:])
            return jnp.concatenate((x1 * cos - x2 * sin, x1 * sin + x2 * cos), axis=-1)
        key = jax.random.key(seed)
        ks = jax.random.split(key, 9)
        B, T = (2, 256)
        s = 1.0 / np.sqrt(D_MODEL)
        inp = {'x': jax.random.normal(ks[0], (B, T, D_MODEL), dtype=jnp.float32), 'Wq': jax.random.normal(ks[1], (D_MODEL, D_MODEL), dtype=jnp.float32) * s, 'bq': jnp.zeros((D_MODEL,), dtype=jnp.float32), 'Wk': jax.random.normal(ks[2], (D_MODEL, D_MODEL), dtype=jnp.float32) * s, 'bk': jnp.zeros((D_MODEL,), dtype=jnp.float32), 'Wv': jax.random.normal(ks[3], (D_MODEL, D_MODEL), dtype=jnp.float32) * s, 'bv': jnp.zeros((D_MODEL,), dtype=jnp.float32), 'Wo': jax.random.normal(ks[4], (D_MODEL, D_MODEL), dtype=jnp.float32) * s, 'bo': jnp.zeros((D_MODEL,), dtype=jnp.float32)}
        return inp
    _L1_attn_b_in = _L1_attn_b_setup()

    def _L1_ffn_setup():
        import jax, jax.numpy as jnp
        import numpy as np
        R = 64
        key = jax.random.key(seed)
        k1, k2, k3 = jax.random.split(key, 3)
        B, S, D_IN, D_OUT = (8, 512, 128, 128)
        x = jax.random.normal(k1, (B, S, D_IN), dtype=jnp.float32)
        weight = jax.random.normal(k2, (D_OUT, D_IN), dtype=jnp.float32) * (1.0 / np.sqrt(D_IN))
        disha = jax.random.normal(k3, (R, D_OUT), dtype=jnp.float32) * 0.01
        return {'x': x, 'weight': weight, 'disha': disha}
    _L1_ffn_in = _L1_ffn_setup()
    _d = {'L0_attn_a_x': _L0_attn_a_in['x'], 'L0_attn_a_Wqkv': _L0_attn_a_in['Wqkv'], 'L0_attn_a_bqkv': _L0_attn_a_in['bqkv'], 'L0_attn_a_Wo': _L0_attn_a_in['Wo'], 'L0_attn_a_bo': _L0_attn_a_in['bo'], 'L0_attn_b_Wqkv': _L0_attn_b_in['Wqkv'], 'L0_attn_b_bqkv': _L0_attn_b_in['bqkv'], 'L0_attn_b_r_sigma': _L0_attn_b_in['r_sigma'], 'L0_attn_b_Wproj': _L0_attn_b_in['Wproj'], 'L0_attn_b_bproj': _L0_attn_b_in['bproj'], 'L0_ffn_W': _L0_ffn_in['W'], 'L0_ffn_b': _L0_ffn_in['b'], 'L0_ffn_logits': _L0_ffn_in['logits'], 'L0_ffn_u': _L0_ffn_in['u'], 'L1_attn_a_Wq': _L1_attn_a_in['Wq'], 'L1_attn_a_Wk': _L1_attn_a_in['Wk'], 'L1_attn_a_Wv': _L1_attn_a_in['Wv'], 'L1_attn_a_u': _L1_attn_a_in['u'], 'L1_attn_a_v': _L1_attn_a_in['v'], 'L1_attn_a_Wo': _L1_attn_a_in['Wo'], 'L1_attn_a_bo': _L1_attn_a_in['bo'], 'L1_attn_b_Wq': _L1_attn_b_in['Wq'], 'L1_attn_b_bq': _L1_attn_b_in['bq'], 'L1_attn_b_Wk': _L1_attn_b_in['Wk'], 'L1_attn_b_bk': _L1_attn_b_in['bk'], 'L1_attn_b_Wv': _L1_attn_b_in['Wv'], 'L1_attn_b_bv': _L1_attn_b_in['bv'], 'L1_attn_b_Wo': _L1_attn_b_in['Wo'], 'L1_attn_b_bo': _L1_attn_b_in['bo'], 'L1_ffn_weight': _L1_ffn_in['weight'], 'L1_ffn_disha': _L1_ffn_in['disha']}
    _x0 = _d['L0_attn_a_x']
    _d['L0_attn_a_x'] = jax.random.normal(jax.random.fold_in(jax.random.key(seed), 1), (4, 1024, 128), dtype=_x0.dtype)
    del _x0
    return _d

def reference(L0_attn_a_x, L0_attn_a_Wqkv, L0_attn_a_bqkv, L0_attn_a_Wo, L0_attn_a_bo, L0_attn_b_Wqkv, L0_attn_b_bqkv, L0_attn_b_r_sigma, L0_attn_b_Wproj, L0_attn_b_bproj, L0_ffn_W, L0_ffn_b, L0_ffn_logits, L0_ffn_u, L1_attn_a_Wq, L1_attn_a_Wk, L1_attn_a_Wv, L1_attn_a_u, L1_attn_a_v, L1_attn_a_Wo, L1_attn_a_bo, L1_attn_b_Wq, L1_attn_b_bq, L1_attn_b_Wk, L1_attn_b_bk, L1_attn_b_Wv, L1_attn_b_bv, L1_attn_b_Wo, L1_attn_b_bo, L1_ffn_weight, L1_ffn_disha):

    def _L0_attn_a_ref(x, Wqkv, bqkv, Wo, bo):
        import jax, jax.numpy as jnp
        import numpy as np
        B, T, C = (2, 256, 128)
        H = 16
        D = C // H
        SCALE = 1.0 / np.sqrt(D)
        Bsz, Tlen, Cdim = x.shape
        qkv = x @ Wqkv + bqkv
        qkv = qkv.reshape(Bsz, Tlen, 3, H, D)
        qkv = jnp.transpose(qkv, (2, 0, 3, 1, 4))
        q, k, v = (qkv[0], qkv[1], qkv[2])
        att = jnp.einsum('bhqd,bhkd->bhqk', q, k) * SCALE
        i = jnp.arange(Tlen)
        mask = i[None, :] >= i[:, None]
        att = jnp.where(mask[None, None], att, -jnp.inf)
        att = jax.nn.softmax(att, axis=-1)
        y = jnp.einsum('bhqk,bhkd->bhqd', att, v)
        y = jnp.transpose(y, (0, 2, 1, 3)).reshape(Bsz, Tlen, Cdim)
        y = y @ Wo + bo
        return y

    def _L0_attn_b_ref(x, Wqkv, bqkv, r_sigma, Wproj, bproj):
        import jax, jax.numpy as jnp
        import numpy as np
        B, T, C = (2, 256, 128)
        DIM, H = (128, 16)
        HD = DIM // H
        b, t, c = x.shape
        qkv = x @ Wqkv + bqkv
        qkv = qkv.reshape(b, t, 3, H, HD).transpose(2, 0, 3, 1, 4)
        q, k, v = (qkv[0], qkv[1], qkv[2])
        qn = jnp.sum(q * q, axis=-1)
        kn = jnp.sum(k * k, axis=-1)
        dot = jnp.einsum('bhid,bhjd->bhij', k, q)
        dist2 = kn[..., :, None] + qn[..., None, :] - 2.0 * dot
        Kmat = jnp.exp(-dist2 * r_sigma)
        out = jnp.einsum('bhij,bhjd->bhid', Kmat, v)
        out = out.transpose(0, 2, 1, 3).reshape(b, t, DIM)
        return out @ Wproj + bproj

    def _L0_ffn_ref(x, W, b, logits, u):
        import jax, jax.numpy as jnp
        import numpy as np
        NUM_OPS, B, T, D = (8, 8, 64, 128)
        gumbel = -jnp.log(-jnp.log(u))
        idx = jnp.argmax(jax.nn.log_softmax(logits) + gumbel)
        out = jnp.einsum('btd,de->bte', x, W[idx]) + b[idx]
        return out

    def _L1_attn_a_ref(x, Wq, Wk, Wv, u, v, Wo, bo):
        import jax, jax.numpy as jnp
        import numpy as np
        NUM_HEADS = 16

        def _sinusoid_rel_pos(seq_len, dim):
            pos = jnp.arange(seq_len - 1, -1, -1, dtype=jnp.float32)
            inv_freq = 1.0 / 10000.0 ** (jnp.arange(0, dim, 2, dtype=jnp.float32) / dim)
            ang = pos[:, None] * inv_freq[None, :]
            return jnp.concatenate([jnp.sin(ang), jnp.cos(ang)], axis=-1)

        def _rel_shift(x):
            B, H, S, L = x.shape
            x = jnp.pad(x, ((0, 0), (0, 0), (0, 0), (1, 0)))
            x = x.reshape(B, H, L + 1, S)
            return x[:, :, 1:S + 1, :]
        B, S, C = x.shape
        H = NUM_HEADS
        dk = Wq.shape[1] // H
        dv = Wv.shape[1] // H
        Q = (x @ Wq).reshape(B, S, H, dk).transpose(0, 2, 1, 3)
        K = (x @ Wk).reshape(B, S, H, dk).transpose(0, 2, 1, 3)
        V = (x @ Wv).reshape(B, S, H, dv).transpose(0, 2, 1, 3)
        r = _sinusoid_rel_pos(S, dk)
        term1 = jnp.einsum('bhqd,bhkd->bhqk', Q, K)
        term2 = jnp.einsum('bhqd,kd->bhqk', Q, r)
        term3 = jnp.einsum('hd,bhkd->bhk', u, K)[:, :, None, :]
        term4 = jnp.einsum('hd,kd->hk', v, r)[None, :, None, :]
        scores = (term1 + term3 + _rel_shift(term2 + term4)) / jnp.sqrt(jnp.asarray(dk, dtype=x.dtype))
        attn = jax.nn.softmax(scores, axis=-1)
        out = jnp.einsum('bhqk,bhkd->bqhd', attn, V).reshape(B, S, H * dv)
        return out @ Wo + bo

    def _L1_attn_b_ref(x, Wq, bq, Wk, bk, Wv, bv, Wo, bo):
        import jax, jax.numpy as jnp
        import numpy as np
        D_MODEL = 128
        NUM_HEADS = 16
        HEAD_DIM = D_MODEL // NUM_HEADS

        def _rope(x):
            B, H, T, d = x.shape
            pos = jnp.arange(T, dtype=x.dtype)[:, None]
            freq_seq = jnp.arange(d // 2, dtype=x.dtype)
            inv_freq = 1.0 / 10000.0 ** (freq_seq / (d // 2))
            ang = pos * inv_freq[None, :]
            sin = jnp.sin(ang)[None, None]
            cos = jnp.cos(ang)[None, None]
            x1, x2 = (x[..., :d // 2], x[..., d // 2:])
            return jnp.concatenate((x1 * cos - x2 * sin, x1 * sin + x2 * cos), axis=-1)
        B, T, _ = x.shape

        def proj(W, b):
            return (x @ W + b).reshape(B, T, NUM_HEADS, HEAD_DIM).transpose(0, 2, 1, 3)
        q = _rope(proj(Wq, bq))
        k = _rope(proj(Wk, bk))
        v = proj(Wv, bv)
        scores = jnp.einsum('bhqd,bhkd->bhqk', q, k) / jnp.sqrt(jnp.asarray(HEAD_DIM, dtype=x.dtype))
        attn = jax.nn.softmax(scores, axis=-1)
        ctx = jnp.einsum('bhqk,bhkd->bhqd', attn, v)
        ctx = ctx.transpose(0, 2, 1, 3).reshape(B, T, D_MODEL)
        return ctx @ Wo + bo

    def _L1_ffn_ref(x, weight, disha):
        import jax, jax.numpy as jnp
        import numpy as np
        R = 64
        result = jnp.einsum('bsd,od->bso', x, weight)
        r = disha.shape[0]
        pooled = x.reshape(*x.shape[:-1], x.shape[-1] // r, r).sum(axis=-2)
        return result + pooled @ disha
    x = L0_attn_a_x
    x = x + _L0_attn_a_ref(_layernorm(x, axis=-1), L0_attn_a_Wqkv, L0_attn_a_bqkv, L0_attn_a_Wo, L0_attn_a_bo)
    x = x + _L0_ffn_ref(_layernorm(x, axis=-1), L0_ffn_W, L0_ffn_b, L0_ffn_logits, L0_ffn_u)
    x = x + _L0_attn_b_ref(_layernorm(x, axis=-1), L0_attn_b_Wqkv, L0_attn_b_bqkv, L0_attn_b_r_sigma, L0_attn_b_Wproj, L0_attn_b_bproj)
    x = x + _L0_ffn_ref(_layernorm(x, axis=-1), L0_ffn_W, L0_ffn_b, L0_ffn_logits, L0_ffn_u)
    x = x + _L1_attn_a_ref(_layernorm(x, axis=-1), L1_attn_a_Wq, L1_attn_a_Wk, L1_attn_a_Wv, L1_attn_a_u, L1_attn_a_v, L1_attn_a_Wo, L1_attn_a_bo)
    x = x + _L1_ffn_ref(_layernorm(x, axis=-1), L1_ffn_weight, L1_ffn_disha)
    x = x + _L1_attn_b_ref(_layernorm(x, axis=-1), L1_attn_b_Wq, L1_attn_b_bq, L1_attn_b_Wk, L1_attn_b_bk, L1_attn_b_Wv, L1_attn_b_bv, L1_attn_b_Wo, L1_attn_b_bo)
    x = x + _L1_ffn_ref(_layernorm(x, axis=-1), L1_ffn_weight, L1_ffn_disha)
    return x

_drawn_inputs = setup_inputs


def setup_inputs(seed=0):
    import zlib

    import numpy as np

    out = dict(_drawn_inputs(seed))
    spreads = {'L0_attn_a_bqkv': (0.0, 0.1),
     'L0_attn_a_bo': (0.0, 0.1),
     'L0_attn_b_bqkv': (0.0, 0.1),
     'L0_attn_b_bproj': (0.0, 2.0),
     'L0_ffn_b': (0.0, 0.1),
     'L1_attn_a_bo': (0.0, 2.0),
     'L1_attn_b_bq': (0.0, 2.0),
     'L1_attn_b_bk': (0.0, 2.0),
     'L1_attn_b_bv': (0.0, 2.0),
     'L1_attn_b_bo': (0.0, 2.0)}
    factors = {'L0_attn_a_Wqkv': 4.168,
     'L1_attn_a_Wq': 63.937,
     'L1_attn_a_Wk': 57.551,
     'L1_attn_a_Wv': 8.0,
     'L1_attn_a_u': 200.0,
     'L1_attn_a_v': 200.0,
     'L1_attn_a_Wo': 8.0,
     'L1_attn_b_Wq': 200.0,
     'L1_attn_b_Wk': 200.0,
     'L1_ffn_disha': 8.0}
    for name, (base, spread) in spreads.items():
        noise = np.random.default_rng([zlib.crc32(name.encode()), seed]).standard_normal(out[name].shape)
        drawn = base * np.exp(spread * noise) if base else spread * noise
        out[name] = jnp.asarray(drawn.astype(out[name].dtype))
    for name, factor in factors.items():
        out[name] = (out[name] * factor).astype(out[name].dtype)
    return out
```

```python
from contextlib import ExitStack

import numpy as np

import concourse.bass as bass
from concourse import mybir

F32 = mybir.dt.float32
BF16 = mybir.dt.bfloat16
U16 = mybir.dt.uint16
ALU = mybir.AluOpType
ACT = mybir.ActivationFunctionType
AX = mybir.AxisListType

B, T, C, H, D = 4, 1024, 128, 16, 8
P = 128
NT = T // P
HALF = 512
TURN = 4
TURNS = H // TURN
STAGES = 4
MASKED, RBF, REL, ROPE = range(STAGES)
EPS = 1e-5
SCALE = float(np.float32(1.0) / np.sqrt(np.float32(D)))
NOPS = 8
BIG = -1e30

BASE = 9 * D
RELROWS = 6 * D
QPARTS6, KPARTS6 = (0, 0, 1, 0, 2, 1), (0, 1, 0, 2, 0, 1)
MAXROW = [BASE, None, BASE + RELROWS, BASE]
SROWS = [BASE, None, BASE + RELROWS, BASE]
STROWS = [BASE + 3, BASE + 6, BASE + RELROWS + 3, BASE + 3]
REC = BASE + RELROWS
NLOAD = [2, 3, 5, 2]
NMAXD = [1, 0, 3, 1]


def halves(s, qt):
    lo = qt * P if s == MASKED else 0
    return [(h, max(lo, h * HALF), (h + 1) * HALF) for h in range(2) if lo < (h + 1) * HALF]


def queries(s, kt):
    return (kt + 1) * P if s == MASKED else T


FIRST = [(0, qt) for qt in range(8)] + [(1, qt) for qt in range(4)]
FILL = [sum(len(halves(s, qt)) for _, qt in FIRST) for s in range(STAGES)]
PERTURN = [TURN * sum(len(halves(s, qt)) for qt in range(8)) for s in range(STAGES)]
SOFT = [s != RBF for s in range(STAGES)]
NTURN = B * TURNS


def before(per_stage):
    out, n = [], 0
    for x in per_stage:
        out.append(n)
        n += x
    return out


S0 = before([(FILL[s] + NTURN * PERTURN[s]) * SOFT[s] for s in range(STAGES)])
M0 = before([(1 + B * H) * SOFT[s] for s in range(STAGES)])
W0 = [s * B * H * NT for s in range(STAGES)]
def copies(qt):
    return 3 if qt == 3 else 2


def ahead(j, i):
    return ((j + 1) % TURN, 4 + i) if i < 4 else ((j + 2) % TURN, i - 4)


CPFILL = sum(copies(qt) for _, qt in FIRST)
CP_QK, CP_KQ, CPTURN = {}, {}, 0
for _j in range(TURN):
    for _i in range(NT):
        CP_QK[_j, _i] = CPTURN = CPTURN + copies(ahead(_j, _i)[1])
        CP_KQ[_j, _i] = CPTURN = CPTURN + 2
GROUPS = [6, 10, 8, 10]
G0 = before([B * n for n in GROUPS])
POOLOPS = [8 + 1, 8 + 1 + 2 + 8, 16 + 6, 8 + 6 + 1]
PL0 = before([B * n for n in POOLOPS])
STORES = [18, 18 + 6, 9 + 9 + 6 + 6, 18]
R0 = before([B * n for n in STORES])
SETUP_DVE = 15 + 2 * NOPS + 2
KC = [16 * TURN * n for n in (1, 2, 2, 1)]
AHEAD_ST, AHEAD_EXP, AHEAD_PV, AHEAD_MAX, AHEAD_EV, AHEAD_OUT = 16, 2, 4, 2, 1, 16


def loads_before(s, slot):
    return 16 * sum(NLOAD[r] * (NTURN + (slot < 2)) for r in range(s))


def maxes_before(s, slot):
    return 16 * sum(NMAXD[r] * (NTURN + (slot < 1)) for r in range(s))


def build(nc, a, k, out):
    records_k = nc.dram_tensor("records_k", [2 * H, REC, T], BF16, kind="Internal").ap()
    records_q = nc.dram_tensor("records_q", [2 * H, REC, T], BF16, kind="Internal").ap()
    records_h = nc.dram_tensor("records_h", [2 * H, RELROWS, T], BF16, kind="Internal").ap()
    heads_out = nc.dram_tensor("heads_out", [B * H, P, 2 * P], F32, kind="Internal").ap()

    ctx = ExitStack()
    with ctx:
        def sb(name, shape, dt=F32):
            return ctx.enter_context(nc.sbuf_tensor(name, shape, dt))

        def ps(name, shape):
            return ctx.enter_context(nc.psum_tensor(name, shape, F32))

        def sem(name):
            return ctx.enter_context(nc.semaphore(name))

        x = sb("x", [P, B, NT, C])
        kst = [sb(f"kst{i}", [P, TURN, T], BF16) for i in range(2)]
        qst = [sb(f"qst{i}", [P, TURN, T], BF16) for i in range(2)]
        qst_up = sb("qst_up", [P, TURN, T], BF16)
        qst_zero = sb("qst_zero", [P, TURN, T], BF16)
        probs = sb("probs", [P, 4, T])
        vst = sb("vst", [P, TURN, NT, 32])
        values = sb("values", [P, 2, NT, C])
        osb = sb("osb", [P, TURN, 2 * P])
        oT = sb("oT", [P, T])
        den = sb("den", [P, T])
        xn = sb("xn", [P, NT, C])
        xnT = sb("xnT", [P, T])
        proj = sb("proj", [P, 4, T])
        work = sb("work", [P, 2, T])
        parts = sb("parts", [P, 4, 3, T], BF16)
        norms = parts[0:H, 2:4].rearrange("h a p t -> h (a p t)").bitcast(F32).rearrange("h (a t) -> h a t", a=3)
        nparts = proj[0:H, 1:4].rearrange("h a t -> h (a t)").bitcast(BF16).rearrange("h (m i t) -> h m i t", m=2, i=3)
        pool_flag = sb("pool_flag", [1, 2])
        tables = sb("tables", [P, 4, T])
        stats = sb("stats", [P, NT, 6])
        meanvar = sb("meanvar", [P, NT, 2])
        rstd = sb("rstd", [P, 2, NT])
        half_pow = sb("half_pow", [P, NT])
        mx = sb("mx", [P, TURN, 2 * NT])
        mfull = sb("mfull", [P, 3, NT])
        mparts = sb("mparts", [P, 3, NT], BF16)
        mrow = sb("mrow", [3 * NT, P], BF16)
        wq = sb("wq", [P, STAGES, C])
        wqp = sb("wqp", [P, 2, C])
        wk = sb("wk", [P, STAGES, C])
        wkp = sb("wkp", [P, C])
        wv = sb("wv", [P, STAGES, C])
        wo = sb("wo", [P, STAGES, C])
        wf = sb("wf", [P, 2, C])
        wcand, bcand = (probs[:, i].rearrange("p (e c) -> p e c", e=NOPS) for i in range(2))
        bff = sb("bff", [P, C])
        wadd = sb("wadd", [P, C])
        bo = sb("bo", [P, STAGES, C])
        bv = sb("bv", [P, STAGES, C])
        cols = sb("cols", [P, 16])
        pick = sb("pick", [P, 12, NOPS])
        sig2 = sb("sig2", [P, 2])
        ident = sb("ident", [P, P])
        identb = sb("identb", [P, P], BF16)
        hide_qk = sb("hide_qk", [P, P], BF16)
        hide_kq = sb("hide_kq", [P, P], BF16)
        up_qk = sb("up_qk", [P, P], U16)
        zero_qk = sb("zero_qk", [P, P + 1], U16)
        up_kq = sb("up_kq", [P, P], U16)
        zero_kq = sb("zero_kq", [P, P], U16)
        neghalf = sb("neghalf", [P, H])

        pst = ps("pst", [P, 2, T])
        pmax = ps("pmax", [P, 2, HALF])
        ppv = ps("ppv", [P, HALF])
        pm = ps("pm", [P, HALF])
        pmb = pm[:, :].bitcast(BF16)

        s_c = sem("s_c")
        s_kc = [sem(f"s_kc{i}") for i in range(STAGES)]
        s_ld = [sem(f"s_ld{i}") for i in range(TURN)]
        s_ldm = [sem(f"s_ldm{i}") for i in range(TURN)]
        s_st = sem("s_st")
        s_exp = sem("s_exp")
        s_pv = sem("s_pv")
        s_ev = sem("s_ev")
        s_os = [sem(f"s_os{i}") for i in range(TURN)]
        s_vs = sem("s_vs")
        s_s = sem("s_s")
        s_sm = sem("s_sm")
        s_mc = sem("s_mc")
        s_mt = sem("s_mt")
        s_mr = sem("s_mr")
        s_dg = sem("s_dg")
        s_cp = sem("s_cp")
        s_eld = sem("s_eld")
        s_rc = sem("s_rc")
        s_at = sem("s_at")
        s_xb = sem("s_xb")
        s_ep = sem("s_ep")
        s_ex = sem("s_ex")
        ln = {w: {n: sem(f"s_{w}_{n}") for n in ("stat", "aggr", "eps", "rstd", "xn", "tp", "xt")} for w in "fa"}
        s_fb = sem("s_fb")
        s_fp = sem("s_fp")
        s_fx = sem("s_fx")
        s_pp = sem("s_pp")
        s_pe = sem("s_pe")
        s_va = sem("s_va")
        s_pl = sem("s_pl")
        s_rec = sem("s_rec")
        s_tab = sem("s_tab")
        s_x = sem("s_x")
        s_top = sem("s_top")
        s_dv = sem("s_dv")
        s_ac = sem("s_ac")
        s_held = sem("s_held")
        s_fin = sem("s_fin")

        def soft_heads(s):
            return kst[s % 2], qst[s % 2]

        block = ctx.enter_context(nc.Block())

        def hold(eng, q, value):
            eng.wait_ge(q, value)
            if not isinstance(value, int):
                eng.sem_inc(s_held, 1)

        NCONST = [0]

        @block.sync
        def _(sp):
            def const(dst, src):
                sp.dma_start(dst, src).then_inc(s_c, 16)
                NCONST[0] += 16

            for b in range(B):
                sp.dma_start(x[:, b], a["L0_attn_a_x"][b].rearrange("(t p) c -> p t c", p=P)).then_inc(s_x, 16)

            def rowb(v, n=P):
                return v.rearrange("(o c) -> o c", o=1).to_broadcast([n, v.shape[0]])

            for s, (w, bias) in enumerate((("L0_attn_a_Wqkv", "L0_attn_a_bqkv"), ("L0_attn_b_Wqkv", "L0_attn_b_bqkv"))):
                for n, t in enumerate((wq, wk, wv)):
                    const(t[:, s], a[w][:, n * C:(n + 1) * C])
                const(cols[:, 2 * s:2 * s + 1], a[bias][0:C].rearrange("(c o) -> c o", o=1))
                const(cols[:, 2 * s + 1:2 * s + 2], a[bias][C:2 * C].rearrange("(c o) -> c o", o=1))
                const(bv[:, s], rowb(a[bias][2 * C:3 * C]))
            for s, n in ((2, "L1_attn_a"), (3, "L1_attn_b")):
                const(wq[:, s], a[n + "_Wq"])
                const(wk[:, s], a[n + "_Wk"])
                const(wv[:, s], a[n + "_Wv"])
            const(wqp[:, 0], k["Wq_a_swapped"])
            const(wqp[:, 1], k["Wq_b_swapped"])
            const(wkp[:, :], k["Wk_b_swapped"])
            for n, v in ((4, a["L1_attn_a_u"]), (5, a["L1_attn_a_v"]), (6, k["v_swapped"])):
                const(cols[:, n:n + 1], v.rearrange("h (d o) -> (h d) o", o=1))
            for n, v in ((7, a["L1_attn_b_bq"]), (8, a["L1_attn_b_bk"]), (9, k["bq_swapped"]), (10, k["bk_swapped"])):
                const(cols[:, n:n + 1], v.rearrange("(c o) -> c o", o=1))
            const(bv[:, 3], rowb(a["L1_attn_b_bv"]))
            for s, (w, bias) in enumerate((("L0_attn_a_Wo", "L0_attn_a_bo"), ("L0_attn_b_Wproj", "L0_attn_b_bproj"),
                                           ("L1_attn_a_Wo", "L1_attn_a_bo"), ("L1_attn_b_Wo", "L1_attn_b_bo"))):
                const(wo[:, s], a[w])
                const(bo[:, s], rowb(a[bias]))
            const(wcand, a["L0_ffn_W"].rearrange("e c n -> c e n"))
            const(bcand, a["L0_ffn_b"].rearrange("(o e) n -> o e n", o=1).to_broadcast([P, NOPS, C]))
            const(pick[:, 0], rowb(a["L0_ffn_logits"]))
            const(pick[:, 1], rowb(a["L0_ffn_u"]))
            const(pick[:, 2], rowb(k["rank"]))
            const(wf[:, 1], k["ffn_weight_T"])
            const(wadd[:, :], k["disha_twice"])
            const(sig2[:, 0:1], a["L0_attn_b_r_sigma"].to_broadcast([P, 1]))
            const(ident[:, :], k["ident"])
            const(neghalf[:, :], k["neghalf"])
            for dst, n in ((identb, "ident_bf"), (hide_qk, "hide_qk"), (hide_kq, "hide_kq")):
                const(dst[:, :], k[n].bitcast(BF16))
            for dst, n in ((up_qk, "up_qk"), (zero_qk, "zero_qk"), (up_kq, "up_kq"), (zero_kq, "ident_int")):
                const(dst[:, :], k[n])
            for n in range(4):
                const(tables[:, n], k["tables"][n])

            def const_rows(s):
                keys, qs = soft_heads(s)
                r = MAXROW[s]
                for slot in range(TURN):
                    if s == RBF:
                        sp.dma_start(keys[BASE + 3:BASE + 6, slot], k["ones3"].bitcast(BF16)).then_inc(s_kc[s], 16)
                        sp.dma_start(qs[BASE:BASE + 3, slot], k["ones3"].bitcast(BF16)).then_inc(s_kc[s], 16)
                    else:
                        sp.dma_start(keys[r:r + 3, slot], k["minus3"].bitcast(BF16)).then_inc(s_kc[s], 16)
                    if s == REL:
                        sp.dma_start(keys[BASE:REC, slot], k["rel_rows"].bitcast(BF16)).then_inc(s_kc[s], 16)

            def load(s, slot, rec):
                keys, qs = soft_heads(s)
                if s == RBF:
                    pairs = [(keys[0:BASE + 3, slot], records_k[rec, 0:BASE + 3]),
                             (qs[0:BASE, slot], records_q[rec, 0:BASE]),
                             (qs[BASE + 3:BASE + 6, slot], records_q[rec, BASE:BASE + 3])]
                elif s == REL:
                    pairs = [(keys[0:BASE, slot], records_k[rec, 0:BASE]),
                             (qs[0:REC, slot], records_q[rec, 0:REC]),
                             (qst_up[0:BASE, slot], records_q[rec, 0:BASE]),
                             (qst_up[BASE:REC, slot, 0:T - 1], records_h[rec, :, 1:T]),
                             (qst_zero[0:BASE, slot], records_q[rec, 0:BASE])]
                else:
                    pairs = [(keys[0:BASE, slot], records_k[rec, 0:BASE]), (qs[0:BASE, slot], records_q[rec, 0:BASE])]
                for dst, src in pairs:
                    sp.dma_start(dst, src).then_inc(s_ld[slot], 16)

            def place_max(s, slot, count):
                sp.wait_ge(s_mr, count)
                r = MAXROW[s]
                for dst in ([qst[s % 2]] if s != REL else [qst[0], qst_up, qst_zero]):
                    sp.dma_start(dst[r:r + 3, slot], mrow[:, :]).then_inc(s_ldm[slot], 16)

            def store_records(s, b, par):
                done = PL0[s] + b * POOLOPS[s]
                lo = par * H
                def rows(t, r, src):
                    sp.dma_start(t[bass.ds(lo, H), r:r + D], src).then_inc(s_rec, 16)
                sp.wait_ge(s_pl, done + POOLOPS[s])
                for i in range(3):
                    for j in range(3):
                        rows(records_k, (3 * i + j) * D, parts[:, 0, j])
                        rows(records_q, (3 * i + j) * D, parts[:, 1, i])
                if s == REL:
                    for i, p in enumerate(QPARTS6):
                        rows(records_q, BASE + i * D, parts[:, 2, p])
                        rows(records_h, i * D, parts[:, 3, p])
                if s == RBF:
                    for i in range(3):
                        sp.dma_start(records_k[bass.ds(lo, H), BASE + i], nparts[:, 0, i]).then_inc(s_rec, 16)
                        sp.dma_start(records_q[bass.ds(lo, H), BASE + i], nparts[:, 1, i]).then_inc(s_rec, 16)

            def load_outputs(s, b, kE):
                if not isinstance(kE, int) or kE > 0:
                    sp.wait_ge(s_ep, 2 * kE)
                for j in range(TURN):
                    sp.wait_ge(s_os[j], 16 * (NTURN * s + TURNS * b + TURNS) + AHEAD_OUT)
                o = heads_out[bass.ds(b * H, H)]
                for g in range(4):
                    q = slice(g * 2 * P, (g + 1) * 2 * P)
                    sp.dma_start(oT[:, q], o[:, 32 * g:32 * g + D]).then_inc(s_eld, 16)
                    sp.dma_start(den[:, q], o[:, 32 * g + D:32 * g + D + 1].to_broadcast([H, D, 2 * P])).then_inc(s_eld, 16)

            const_rows(0)
            for s in range(STAGES):
                if s == 0:
                    store_records(0, 0, 0)
                sp.wait_ge(s_rec, 16 * (R0[s] + STORES[s]))
                if s + 1 < STAGES:
                    if s + 1 >= 2:
                        sp.wait_ge(s_st, W0[s] + AHEAD_ST)
                        for n in range(2):
                            sp.wait_ge(s_ld[n], loads_before(s, n))
                        if SOFT[s - 1]:
                            sp.wait_ge(s_ldm[0], maxes_before(s, 0))
                    const_rows(s + 1)
                for n in range(2):
                    sp.wait_ge(s_st, W0[s] + AHEAD_ST)
                    load(s, n, n)
                if SOFT[s]:
                    place_max(s, 0, M0[s] + 1)
                with sp.Fori(0, B) as b, sp.Fori(0, TURNS) as c:
                    g = b * TURNS + c
                    if s > 0:
                        with sp.If(c == 0):
                            with sp.If(b < B - 1):
                                load_outputs(s - 1, (b + 1) % B, 4 * s + b - 3)
                    with sp.If(c == 0):
                        with sp.If(b == B - 1):
                            load_outputs(s, 0, 4 * s)
                    if s == REL:
                        with sp.If(g == NTURN - TURNS):
                            sp.wait_ge(s_pl, PL0[ROPE])
                            for n in range(2):
                                sp.dma_start(tables[:, n], k["tables"][4 + n]).then_inc(s_tab, 16)
                    with sp.If(c == TURNS - 1):
                        with sp.If(b < B - 1):
                            store_records(s, (b + 1) % B, (b + 1) % 2)
                        if s + 1 < STAGES:
                            with sp.If(b == B - 1):
                                store_records(s + 1, 0, 0)
                    for j in range(TURN):
                        if j == 2:
                            with sp.If(c == TURNS - 1):
                                with sp.If(b < B - 1):
                                    hold(sp, s_rec, 16 * (R0[s] + (b + 2) * STORES[s]))
                                if s + 1 < STAGES:
                                    with sp.If(b == B - 1):
                                        sp.wait_ge(s_rec, 16 * (R0[s + 1] + STORES[s + 1]))
                        sp.wait_ge(s_st, W0[s] + NT * (TURN * g + j - 1) + AHEAD_ST)
                        load(s, (j + 2) % TURN, (g * TURN + (j + 2)) % (2 * H))
                        if j:
                            sp.wait_ge(s_ev, B * H * s + TURN * g + j + AHEAD_EV)
                            sp.dma_start(heads_out[g * TURN + (j - 1)], osb[:, j - 1]).then_inc(s_os[j - 1], 16)
                        if SOFT[s]:
                            place_max(s, (j + 1) % TURN, M0[s] + TURN * g + j + 2)
                    sp.wait_ge(s_ev, B * H * s + TURN * g + TURN + AHEAD_EV)
                    sp.dma_start(heads_out[g * TURN + (TURN - 1)], osb[:, TURN - 1]).then_inc(s_os[TURN - 1], 16)
            for b in range(1, B):
                load_outputs(STAGES - 1, b, 4 * (STAGES - 1) + b)
            for b in range(B):
                sp.wait_ge(s_fx, 2 * (4 * (STAGES - 1) + b + 1))
                sp.dma_start(out[b].rearrange("(t p) c -> p t c", p=P), x[:, b]).then_inc(s_fin, 16)
            sp.wait_ge(s_fin, 16 * B)
            for n in range(2):
                sp.wait_ge(s_ld[n], loads_before(STAGES, n))
            sp.wait_ge(s_ldm[0], maxes_before(STAGES, 0))

        @block.tensor
        def _(pe):
            def scores_qk(s, slot, qt, v, n):
                keys, qs = soft_heads(s)
                R = SROWS[s]
                q = slice(qt * P, (qt + 1) * P)
                for h, lo, hi in halves(s, qt):
                    pe.wait_ge(s_sm, v + (n + 1))
                    bank = pmax[:, n % 2]
                    if s == REL:
                        cut = min(max((qt + 1) * P, lo), hi)
                        segs = [(qst[0], lo, cut), (qst_up, cut, hi)]
                        for qq, p0, p1 in segs:
                            if p1 > p0:
                                mm = pe.matmul(bank[:, p0 - h * HALF:p1 - h * HALF], qq[0:R, slot, q],
                                               keys[0:R, slot, p0:p1], start=True, stop=True)
                    else:
                        diag = s == MASKED and lo == qt * P
                        mm = pe.matmul(bank[:, lo - h * HALF:hi - h * HALF], qs[0:R, slot, q], keys[0:R, slot, lo:hi],
                                       start=True, stop=not diag)
                        if diag:
                            mm = pe.matmul(bank[:, lo - h * HALF:lo - h * HALF + P], identb[:, :], hide_qk[:, :],
                                           start=False, stop=True)
                    mm.then_inc(s_s, 1)
                    n += 1
                return n

            def diag_qk(slot, qt):
                q = slice(qt * P, (qt + 1) * P)
                n = P + 1 if qt < NT - 1 else P
                pe.matmul(pm[:, 0:P], qst_up[0:REC, slot, q], kst[0][0:REC, slot, q], start=True, stop=True)
                pe.matmul(pm[:, P:P + n], qst[0][0:BASE, slot, q], kst[0][0:BASE, slot, qt * P:qt * P + n],
                          start=True, stop=True).then_inc(s_dg, 1)

            def scores_kq(s, slot, kt, w):
                keys, qs = soft_heads(s)
                R = STROWS[s]
                kk = keys[0:R, slot, kt * P:(kt + 1) * P]
                buf = pst[:, kt % 2]
                pe.wait_ge(s_exp, w - 1 + AHEAD_EXP)
                nq = queries(s, kt)
                for lo in range(0, nq, HALF):
                    hi = min(lo + HALF, nq)
                    if s == REL:
                        cut = min(max(kt * P, lo), hi)
                        for qq, p0, p1 in ((qst_up, lo, cut), (qst[0], cut, hi)):
                            if p1 > p0:
                                mm = pe.matmul(buf[:, p0:p1], kk, qq[0:R, slot, p0:p1], start=True, stop=True)
                    else:
                        diag = s == MASKED and hi == nq
                        mm = pe.matmul(buf[:, lo:hi], kk, qs[0:R, slot, lo:hi], start=True, stop=not diag)
                        if diag:
                            mm = pe.matmul(buf[:, nq - P:nq], identb[:, :], hide_kq[:, :], start=False, stop=True)
                mm.then_inc(s_st, 1)

            def diag_kq(slot, kt):
                R = STROWS[REL]
                kk = kst[0][0:R, slot, kt * P:(kt + 1) * P]
                c = 1 if kt == 0 else 0
                pe.matmul(pm[:, 0:P], kk, qst_up[0:R, slot, kt * P:(kt + 1) * P], start=True, stop=True)
                pe.matmul(pm[:, P + c:2 * P], kk, qst_zero[0:R, slot, kt * P - 1 + c:(kt + 1) * P - 1],
                          start=True, stop=True).then_inc(s_dg, 1)

            def pv(s, j, i, w, N):
                kt = NT - 1 - i
                pe.wait_ge(s_exp, w + 1 + AHEAD_EXP)
                if i == 0:
                    pe.wait_ge(s_ev, N + AHEAD_EV)
                    pe.wait_ge(s_vs, N + 1)
                nq = queries(s, kt)
                for g in range(4):
                    n = min(2 * P, nq - g * 2 * P)
                    if n <= 0:
                        continue
                    last = max(0, 2 * g) if s == MASKED else 0
                    mm = pe.matmul(ppv[32 * g:32 * g + 32, 0:n], vst[:, j, kt, :],
                                   probs[:, i % 4, g * 2 * P:g * 2 * P + n],
                                   start=(i == 0), stop=(kt == last), tile_position=(0, 32 * g))
                mm.then_inc(s_pv, 1)

            def turn_max(s, count):
                pe.wait_ge(s_mc, 5 * count)
                pe.transpose(pmb[0:3 * NT, 0:P], mparts[:, :, :].rearrange("p a t -> p (a t)"), identb[:, :]).then_inc(s_mt, 1)

            def layer_norm(w, n):
                for h in range(2):
                    if h == 0:
                        pe.wait_ge(ln[w]["xn"], NT * (n + 1))
                    else:
                        pe.wait_ge(ln[w]["xt"], 2 * n + 1)
                    for t in range(4):
                        mm = pe.transpose(pm[:, t * P:(t + 1) * P], xn[:, 4 * h + t], ident[:, :])
                    mm.then_inc(ln[w]["tp"], 1)
                pe.wait_ge(ln[w]["xt"], 2 * n + 2)

            def finish(s, b, kE):
                pe.wait_ge(s_eld, 128 * (kE + 1))
                if SOFT[s]:
                    pe.wait_ge(s_at, 4 * sum(SOFT[:s]) + b + 1)
                for h in range(2):
                    if h:
                        pe.wait_ge(s_ex, 2 * kE + 1)
                    for t in range(4):
                        mm = pe.matmul(pm[:, t * P:(t + 1) * P], oT[:, (4 * h + t) * P:(4 * h + t + 1) * P], wo[:, s],
                                       start=True, stop=True)
                    mm.then_inc(s_ep, 1)
                pe.wait_ge(s_ex, 2 * kE + 2)
                layer_norm("f", kE)
                for h in range(2):
                    if h:
                        pe.wait_ge(s_fx, 2 * kE + 1)
                    for t in range(4):
                        mm = pe.matmul(pm[:, t * P:(t + 1) * P], xnT[:, (4 * h + t) * P:(4 * h + t + 1) * P], wf[:, s // 2],
                                       start=True, stop=True)
                    mm.then_inc(s_fp, 1)
                pe.wait_ge(s_fx, 2 * kE + 2)

            def start(s, b, kP):
                layer_norm("a", kP)
                n = G0[s] + b * GROUPS[s]
                ws = {0: [wq[:, 0], wk[:, 0]], 1: [wk[:, 1], wq[:, 1]], 2: [wq[:, 2], wqp[:, 0], wk[:, 2]],
                      3: [wq[:, 3], wqp[:, 1], wk[:, 3], wkp[:, :]]}[s]
                for w in ws:
                    for h in range(2):
                        pe.matmul(pm[:, :], w, xnT[:, h * HALF:(h + 1) * HALF], start=True, stop=True).then_inc(s_pp, 1)
                        n = n + 1
                        pe.wait_ge(s_pe, n)
                for h in range(2):
                    for t in range(4):
                        mm = pe.matmul(pm[:, t * P:(t + 1) * P], xnT[:, (4 * h + t) * P:(4 * h + t + 1) * P], wv[:, s],
                                       start=True, stop=True)
                    mm.then_inc(s_pp, 1)
                    n = n + 1
                    pe.wait_ge(s_pe, n)
                if s == RBF:
                    pe.wait_ge(s_pl, PL0[s] + b * POOLOPS[s] + 2)
                    for m in range(2):
                        for h in range(2):
                            pe.matmul(pm[0:H, :], neghalf[:, :], work[:, m, h * HALF:(h + 1) * HALF],
                                      start=True, stop=True).then_inc(s_pp, 1)
                            n = n + 1
                            pe.wait_ge(s_pe, n)

            pe.wait_ge(s_c, NCONST[0])
            pe.wait_ge(s_dv, SETUP_DVE)
            start(0, 0, 0)
            for s in range(STAGES):
                pe.wait_ge(s_kc[s], KC[s])
                v = cp = 0
                if SOFT[s]:
                    for n, qt in FIRST:
                        if qt == 0:
                            pe.wait_ge(s_ld[n], loads_before(s, n) + 16 * NLOAD[s])
                        v = scores_qk(s, n, qt, S0[s], v)
                        if s == REL:
                            if cp:
                                pe.wait_ge(s_cp, cp)
                            if n == 1 and qt == 0:
                                pe.wait_ge(s_mr, M0[s] + 1)
                            diag_qk(n, qt)
                            cp += copies(qt)
                        if n == 0 and qt == 7:
                            if s == REL:
                                pe.wait_ge(s_cp, cp)
                            turn_max(s, M0[s] + 1)
                with pe.Fori(0, B) as b, pe.Fori(0, TURNS) as c:
                    g = b * TURNS + c
                    with pe.If(c == 0):
                        if SOFT[s]:
                            pe.wait_ge(s_mr, M0[s] + TURN * g + 1)
                        if s == REL:
                            pe.wait_ge(s_cp, CPFILL + CPTURN * g)
                        if s > 0:
                            with pe.If(b < B - 1):
                                finish(s - 1, (b + 1) % B, 4 * s + b - 3)
                        with pe.If(b == B - 1):
                            finish(s, 0, 4 * s)
                        pe.nop()
                    with pe.If(c == 1):
                        if SOFT[s]:
                            pe.wait_ge(s_mr, M0[s] + TURN * g + 1)
                        if s == REL:
                            pe.wait_ge(s_cp, CPFILL + CPTURN * g)
                        with pe.If(b < B - 1):
                            start(s, (b + 1) % B, 4 * s + b + 1)
                        if s + 1 < STAGES:
                            with pe.If(b == B - 1):
                                start(s + 1, 0, 4 * s + 4)
                        pe.nop()
                    v0 = S0[s] + FILL[s] + g * PERTURN[s]
                    v = 0
                    w0 = W0[s] + g * NT * TURN
                    cp0 = CPFILL + g * CPTURN
                    for j in range(TURN):
                        n = TURN * g + j
                        for i in range(NT):
                            w = w0 + NT * j + i
                            if SOFT[s]:
                                slot, qt = ahead(j, i)
                                if i == 4:
                                    pe.wait_ge(s_ld[slot], loads_before(s, slot) + 16 * NLOAD[s] * (g + (j + 2) // TURN + 1))
                                v = scores_qk(s, slot, qt, v0, v)
                                if s == REL:
                                    pe.wait_ge(s_cp, cp0 + (CP_QK[j, i] - copies(qt)))
                                    if i == 6:
                                        pe.wait_ge(s_mr, M0[s] + n + 2)
                                    diag_qk(slot, qt)
                            if i == 0:
                                if SOFT[s]:
                                    pe.wait_ge(s_ldm[j], maxes_before(s, j) + 16 * NMAXD[s] * (g + 1))
                                else:
                                    pe.wait_ge(s_ld[j], loads_before(s, j) + 16 * NLOAD[s] * (g + 1))
                            scores_kq(s, j, NT - 1 - i, w)
                            if s == REL:
                                pe.wait_ge(s_cp, cp0 + CP_QK[j, i])
                                diag_kq(j, NT - 1 - i)
                            if SOFT[s] and i == 5:
                                if s == REL:
                                    pe.wait_ge(s_cp, cp0 + CP_KQ[j, i])
                                else:
                                    pe.wait_ge(s_mr, M0[s] + n + 1)
                                turn_max(s, M0[s] + n + 2)
                            if NT * j + i >= 2:
                                jj, ii = divmod(NT * j + i - 2, NT)
                                pv(s, jj, ii, w - 2, B * H * s + TURN * g + jj)
                    for ii in (NT - 2, NT - 1):
                        pv(s, TURN - 1, ii, w0 + NT * (TURN - 1) + ii, B * H * s + TURN * g + TURN - 1)
            pe.wait_ge(s_mr, M0[-1] + 1 + B * H)
            for b in range(1, B):
                finish(STAGES - 1, b, 4 * (STAGES - 1) + b)

        @block.scalar
        def _(act):
            def stage_values(slot, par, h, need=None):
                nc.scalar.activation(vst[:, slot, :, 0:D], values[:, par, :, bass.ds(h * D, D)] if not isinstance(h, int)
                                     else values[:, par, :, h * D:(h + 1) * D], ACT.Copy).then_inc(s_vs, 1)

            def take_out(s, g, j):
                act.wait_ge(s_pv, W0[s] + NT * (TURN * g + j + 1) + AHEAD_PV)
                act.wait_ge(s_os[j], 16 * (NTURN * s + g) + AHEAD_OUT)
                nc.scalar.activation(osb[:, j], ppv[:, 0:2 * P], ACT.Copy).then_inc(s_ev, 1)

            def layer_norm(w, n):
                for h in range(2):
                    act.wait_ge(ln[w]["tp"], 2 * n + h + 1)
                    nc.scalar.activation(xnT[:, h * HALF:(h + 1) * HALF], pm[:, :], ACT.Copy).then_inc(ln[w]["xt"], 1)

            def start(s, b, kP, par):
                layer_norm("a", kP)
                n = G0[s] + b * GROUPS[s]
                if not isinstance(kP, int) or kP > 0:
                    act.wait_ge(s_pl, PL0[s] + b * POOLOPS[s])
                    if s in (RBF, REL):
                        act.wait_ge(s_rec, 16 * (R0[s] + b * STORES[s]))
                dst = {0: [[(1, 0)], [(0, 1)]], 1: [[(1, 3)], [(0, 2)]], 2: [[(1, 4), (2, 5)], [(3, 6)], [(0, None)]],
                       3: [[(1, 7)], [(2, 9)], [(0, 8)], [(3, 10)]]}[s]
                for targets in dst:
                    for h in range(2):
                        n = n + 1
                        act.wait_ge(s_pp, n)
                        for slot, col in targets:
                            o = proj[:, slot, h * HALF:(h + 1) * HALF]
                            if col is None:
                                ins = nc.scalar.activation(o, pm[:, :], ACT.Copy)
                            else:
                                ins = nc.scalar.activation(o, pm[:, :], ACT.Identity, bias=cols[:, col:col + 1])
                        ins.then_inc(s_pe, 1)
                for h in range(2):
                    n = n + 1
                    act.wait_ge(s_pp, n)
                    nc.scalar.activation(values[:, par, 4 * h:4 * h + 4], pm[:, :].rearrange("p (t c) -> p t c", t=4), ACT.Copy)\
                        .then_inc(s_pe, 1)
                if s == RBF:
                    for m in range(2):
                        for h in range(2):
                            n = n + 1
                            act.wait_ge(s_pp, n)
                            nc.scalar.activation(norms[:, m, h * HALF:(h + 1) * HALF], pm[0:H, :], ACT.Copy).then_inc(s_pe, 1)

            act.wait_ge(s_c, NCONST[0])
            nc.scalar.activation(pick[:, 4], pick[:, 1], ACT.Ln).then_inc(s_ac, 1)
            act.wait_ge(s_ac, 1)
            nc.scalar.activation(pick[:, 5], pick[:, 4], ACT.Ln, scale=-1.0).then_inc(s_ac, 1)
            act.wait_ge(s_dv, 7)
            nc.scalar.activation(pick[:, 6], pick[:, 3], ACT.Exp).then_inc(s_ac, 1)
            act.wait_ge(s_dv, 8)
            nc.scalar.activation(pick[:, 8, 0:1], pick[:, 7, 0:1], ACT.Ln).then_inc(s_ac, 1)
            start(0, 0, 0, 0)
            act.wait_ge(s_va, 1)
            for j in range(TURN):
                stage_values(j, 0, j)
            for s in range(STAGES):
                scale = sig2[:, 1:2] if s == RBF else SCALE
                with act.Fori(0, B) as b, act.Fori(0, TURNS) as c:
                    g = b * TURNS + c
                    with act.If(c == 0):
                        if s > 0:
                            with act.If(b < B - 1):
                                layer_norm("f", 4 * s + b - 3)
                        with act.If(b == B - 1):
                            layer_norm("f", 4 * s)
                        act.nop()
                    with act.If(c == 1):
                        with act.If(b < B - 1):
                            start(s, (b + 1) % B, 4 * s + b + 1, (b + 1) % 2)
                        if s + 1 < STAGES:
                            with act.If(b == B - 1):
                                start(s + 1, 0, 4 * s + 4, 0)
                        act.nop()
                    with act.If(c == TURNS - 1):
                        if s + 1 < STAGES:
                            hold(act, s_va, 4 * s + b + 2)
                        else:
                            with act.If(b < B - 1):
                                hold(act, s_va, 4 * s + b + 2)
                        act.nop()
                    w0 = W0[s] + g * NT * TURN
                    nxt = (g + 1) % (2 * TURNS)
                    for j in range(TURN):
                        for i in range(NT):
                            w = w0 + NT * j + i
                            if s == REL:
                                act.wait_ge(s_cp, CPFILL + g * CPTURN + CP_KQ[j, i])
                            else:
                                act.wait_ge(s_st, w + 1 + AHEAD_ST)
                            act.wait_ge(s_pv, w - 3 + AHEAD_PV)
                            nq = queries(s, NT - 1 - i)
                            nc.scalar.activation(probs[:, i % 4, 0:nq], pst[:, (NT - 1 - i) % 2, 0:nq], ACT.Exp,
                                                 scale=scale).then_inc(s_exp, 1)
                            if j and i == 1:
                                take_out(s, g, j - 1)
                                stage_values(j - 1, nxt // TURNS, (nxt % TURNS) * TURN + (j - 1))
                    take_out(s, g, TURN - 1)
                    stage_values(TURN - 1, nxt // TURNS, (nxt % TURNS) * TURN + (TURN - 1))
            for b in range(1, B):
                layer_norm("f", 4 * (STAGES - 1) + b)

        @block.vector
        def _(dve):
            def reduce_qk(s, slot, qt, v, n, cp, dg):
                if s == REL:
                    h = qt // 4
                    at = qt * P - h * HALF
                    to = P + 1 if qt % 4 < 3 else P
                    spans = [(pmax[:, h, at:at + P], up_qk[:, :], pm[:, 0:P]),
                             (pmax[:, h, at:at + to], zero_qk[:, 0:to], pm[:, P:P + to])]
                    if qt == 3:
                        spans.append((pmax[:, 1, 0:1], zero_qk[:, P:P + 1], pm[:, 2 * P:2 * P + 1]))
                    hold(dve, s_dg, dg + 1)
                    for m, (dst, mask, src) in enumerate(spans):
                        dve.copy_predicated(dst, mask, src).then_inc(s_cp, 1)
                        hold(dve, s_cp, cp + (m + 1))
                for h, lo, hi in halves(s, qt):
                    dve.wait_ge(s_s, v + (n + 1))
                    dve.tensor_reduce(mx[:, slot, h * NT + qt:h * NT + qt + 1], pmax[:, n % 2, lo - h * HALF:hi - h * HALF],
                                      AX.X, ALU.max).then_inc(s_sm, 1)
                    n += 1
                return n

            def split_max(slot, count, v):
                n = 5 * (count - 1)
                dve.wait_ge(s_sm, v + AHEAD_MAX)
                dve.tensor_tensor(mfull[:, 0], mx[:, slot, 0:NT], mx[:, slot, NT:2 * NT], ALU.max).then_inc(s_mc, 1)
                dve.wait_ge(s_mc, n + 1)
                dve.tensor_copy(mparts[:, 0], mfull[:, 0]).then_inc(s_mc, 1)
                dve.wait_ge(s_mc, n + 2)
                dve.tensor_tensor(mfull[:, 1], mfull[:, 0], mparts[:, 0], ALU.subtract).then_inc(s_mc, 1)
                dve.wait_ge(s_mc, n + 3)
                dve.tensor_copy(mparts[:, 1], mfull[:, 1]).then_inc(s_mc, 1)
                dve.wait_ge(s_mc, n + 4)
                dve.tensor_tensor(mparts[:, 2], mfull[:, 1], mparts[:, 1], ALU.subtract).then_inc(s_mc, 1)

            def copy_max(s, count, slot, landed):
                dve.wait_ge(s_mt, count)
                if landed is not None:
                    dve.wait_ge(s_ldm[slot], landed)
                dve.tensor_copy(mrow[:, :], pmb[0:3 * NT, 0:P]).then_inc(s_mr, 1)

            def patch_kq(kt, cp, dg):
                buf = pst[:, kt % 2]
                c = 1 if kt == 0 else 0
                hold(dve, s_dg, dg + 1)
                dve.copy_predicated(buf[:, kt * P:(kt + 1) * P], up_kq[:, :], pm[:, 0:P]).then_inc(s_cp, 1)
                hold(dve, s_cp, cp + 1)
                dve.copy_predicated(buf[:, kt * P - 1 + c:(kt + 1) * P - 1], zero_kq[:, c:P], pm[:, P + c:2 * P])\
                    .then_inc(s_cp, 1)

            def layer_norm(w, n, b):
                xb = x[:, b]
                for t in range(NT):
                    dve.bn_stats(stats[:, t], xb[:, t]).then_inc(ln[w]["stat"], 1)
                hold(dve, ln[w]["stat"], NT * (n + 1))
                for t in range(NT):
                    dve.bn_aggr(meanvar[:, t], stats[:, t]).then_inc(ln[w]["aggr"], 1)
                dve.wait_ge(ln[w]["rstd"], n + 1)
                for t in range(NT):
                    dve.tensor_scalar(xn[:, t], xb[:, t], meanvar[:, t, 0:1], rstd[:, 1, t:t + 1], ALU.subtract, ALU.mult)\
                        .then_inc(ln[w]["xn"], 1)

            def finish(s, b, kE):
                xb = x[:, b]
                dve.wait_ge(s_eld, 128 * (kE + 1))
                if SOFT[s]:
                    soft = 4 * sum(SOFT[:s]) + b
                    dve.reciprocal(den[:, :], den[:, :]).then_inc(s_rc, 1)
                    dve.wait_ge(s_rc, soft + 1)
                    dve.tensor_tensor(oT[:, :], oT[:, :], den[:, :], ALU.mult).then_inc(s_at, 1)
                dve.wait_ge(s_xb, kE + 1)
                for h in range(2):
                    dve.wait_ge(s_ep, 2 * kE + h + 1)
                    dve.tensor_tensor(xb[:, 4 * h:4 * h + 4], pm[:, :].rearrange("p (t c) -> p t c", t=4),
                                      xb[:, 4 * h:4 * h + 4], ALU.add).then_inc(s_ex, 1)
                hold(dve, s_ex, 2 * kE + 2)
                layer_norm("f", kE, b)
                if s < 2:
                    dve.wait_ge(s_fb, kE + 1)
                for h in range(2):
                    dve.wait_ge(s_fp, 2 * kE + h + 1)
                    dve.tensor_tensor(xb[:, 4 * h:4 * h + 4], pm[:, :].rearrange("p (t c) -> p t c", t=4),
                                      xb[:, 4 * h:4 * h + 4], ALU.add).then_inc(s_fx, 1)

            dve.memset(vst[:, :, :, :], 0.0).then_inc(s_dv, 1)
            dve.memset(half_pow[:, :], -0.5).then_inc(s_dv, 1)
            dve.memset(mx[:, :, :], 3.0 * BIG).then_inc(s_dv, 1)
            dve.memset(qst_up[:, :, :], 0.0).then_inc(s_dv, 1)
            dve.memset(qst_zero[:, :, :], 0.0).then_inc(s_dv, 1)
            dve.wait_ge(s_dv, 5)
            dve.memset(vst[:, :, :, D:D + 1], 1.0).then_inc(s_dv, 1)
            for q, n in ((s_st, AHEAD_ST), (s_exp, AHEAD_EXP), (s_pv, AHEAD_PV), (s_sm, AHEAD_MAX), (s_ev, AHEAD_EV),
                         *((s_os[j], AHEAD_OUT) for j in range(TURN))):
                dve.sem_inc(q, n)
            dve.wait_ge(s_c, NCONST[0])
            dve.tensor_reduce(pick[:, 7, 1:2], pick[:, 0], AX.X, ALU.max).then_inc(s_top, 1)
            dve.wait_ge(s_top, 1)
            dve.tensor_scalar(pick[:, 3], pick[:, 0], pick[:, 7, 1:2], None, ALU.subtract).then_inc(s_dv, 1)
            dve.wait_ge(s_ac, 3)
            dve.tensor_reduce(pick[:, 7, 0:1], pick[:, 6], AX.X, ALU.add).then_inc(s_dv, 1)
            dve.wait_ge(s_ac, 4)
            dve.tensor_scalar(pick[:, 9], pick[:, 3], pick[:, 8, 0:1], None, ALU.subtract).then_inc(s_dv, 1)
            dve.wait_ge(s_dv, 9)
            dve.tensor_tensor(pick[:, 9], pick[:, 9], pick[:, 5], ALU.subtract).then_inc(s_dv, 1)
            dve.wait_ge(s_dv, 10)
            dve.tensor_reduce(pick[:, 10, 0:1], pick[:, 9], AX.X, ALU.max).then_inc(s_dv, 1)
            dve.wait_ge(s_dv, 11)
            dve.tensor_scalar(pick[:, 11], pick[:, 9], pick[:, 10, 0:1], None, ALU.is_equal).then_inc(s_dv, 1)
            dve.wait_ge(s_dv, 12)
            dve.tensor_tensor(pick[:, 11], pick[:, 11], pick[:, 2], ALU.mult).then_inc(s_dv, 1)
            dve.wait_ge(s_dv, 13)
            dve.tensor_reduce(pick[:, 10, 0:1], pick[:, 11], AX.X, ALU.max).then_inc(s_dv, 1)
            dve.wait_ge(s_dv, 14)
            dve.tensor_scalar(pick[:, 11], pick[:, 2], pick[:, 10, 0:1], None, ALU.is_equal).then_inc(s_dv, 1)
            dve.wait_ge(s_dv, 15)
            dve.tensor_scalar(wf[:, 0], wcand[:, 0], pick[:, 11, 0:1], None, ALU.mult).then_inc(s_dv, 1)
            dve.tensor_scalar(bff[:, :], bcand[:, 0], pick[:, 11, 0:1], None, ALU.mult).then_inc(s_dv, 1)
            for e in range(1, NOPS):
                dve.wait_ge(s_dv, 15 + 2 * e)
                for dst, src in ((wf[:, 0], wcand[:, e]), (bff[:, :], bcand[:, e])):
                    dve.scalar_tensor_tensor(out=dst, in0=src, scalar=pick[:, 11, e:e + 1], in1=dst, op0=ALU.mult,
                                             op1=ALU.add).then_inc(s_dv, 1)
            dve.tensor_tensor(wf[:, 1], wf[:, 1], wadd[:, :], ALU.add).then_inc(s_dv, 1)
            dve.tensor_scalar(sig2[:, 1:2], sig2[:, 0:1], 2.0, None, ALU.mult).then_inc(s_dv, 1)
            dve.wait_ge(s_x, 16 * B)
            layer_norm("a", 0, 0)
            for s in range(STAGES):
                v = cp = 0
                if SOFT[s]:
                    for m, (n, qt) in enumerate(FIRST):
                        v = reduce_qk(s, n, qt, S0[s], v, cp, m)
                        cp += copies(qt)
                        if n == 0 and qt == 7:
                            split_max(0, M0[s] + 1, S0[s] + v)
                            copy_max(s, M0[s] + 1, 0, maxes_before(s, 0) or None)
                with dve.Fori(0, B) as b, dve.Fori(0, TURNS) as c:
                    g = b * TURNS + c
                    with dve.If(c == 0):
                        if s > 0:
                            with dve.If(b < B - 1):
                                finish(s - 1, (b + 1) % B, 4 * s + b - 3)
                        with dve.If(b == B - 1):
                            finish(s, 0, 4 * s)
                        dve.nop()
                    with dve.If(c == 1):
                        with dve.If(b < B - 1):
                            if s > 0:
                                hold(dve, s_fx, 2 * (4 * s + b - 3) + 2)
                            layer_norm("a", 4 * s + b + 1, (b + 1) % B)
                        if s + 1 < STAGES:
                            with dve.If(b == B - 1):
                                dve.wait_ge(s_fx, 2 * 4 * s + 2)
                                layer_norm("a", 4 * s + 4, 0)
                        dve.nop()
                    v0 = S0[s] + FILL[s] + g * PERTURN[s]
                    v = 0
                    cp0 = CPFILL + g * CPTURN
                    dg0 = len(FIRST) + 2 * NT * TURN * g
                    for j in range(TURN):
                        n = TURN * g + j
                        for i in range(NT):
                            if not SOFT[s]:
                                continue
                            slot, qt = ahead(j, i)
                            v = reduce_qk(s, slot, qt, v0, v, cp0 + (CP_QK[j, i] - copies(qt)), dg0 + 2 * (NT * j + i))
                            if i == 3:
                                split_max(slot, M0[s] + n + 2, v0 + v)
                            if s == REL:
                                patch_kq(NT - 1 - i, cp0 + CP_QK[j, i], dg0 + (2 * (NT * j + i) + 1))
                            if i == 5:
                                copy_max(s, M0[s] + n + 2, j, maxes_before(s, j) + 16 * NMAXD[s] * (g + 1))
            for b in range(1, B):
                finish(STAGES - 1, b, 4 * (STAGES - 1) + b)

        @block.gpsimd
        def _(pool):
            def inverse_deviation(w, n):
                hold(pool, ln[w]["aggr"], NT * (n + 1))
                pool.tensor_scalar(rstd[:, 0], meanvar[:, :, 1], EPS, 1.0, ALU.add, ALU.mult).then_inc(ln[w]["eps"], 1)
                hold(pool, ln[w]["eps"], n + 1)
                pool.tensor_tensor(rstd[:, 1], rstd[:, 0], half_pow[:, :], ALU.pow).then_inc(ln[w]["rstd"], 1)

            def wide(row):
                return row.unsqueeze(1).to_broadcast([P, NT, C])

            def finish(s, b, kE):
                xb = x[:, b]
                pool.tensor_tensor(xb, xb, wide(bo[:, s]), ALU.add).then_inc(s_xb, 1)
                inverse_deviation("f", kE)
                if s < 2:
                    hold(pool, ln["f"]["xn"], NT * (kE + 1))
                    pool.tensor_tensor(xb, xb, wide(bff[:, :]), ALU.add).then_inc(s_fb, 1)

            def start(s, b, kP, par):
                inverse_deviation("a", kP)
                base = PL0[s] + b * POOLOPS[s]
                n = [0]

                def step(ins):
                    ins.then_inc(s_pl, 1)
                    n[0] += 1
                    hold(pool, s_pl, base + n[0])

                def split(src, dst, rest):
                    step(pool.tensor_copy(dst[:, 0], src))
                    step(pool.tensor_tensor(rest, src, dst[:, 0], ALU.subtract))
                    step(pool.tensor_copy(dst[:, 1], rest))
                    step(pool.tensor_tensor(dst[:, 2], rest, dst[:, 1], ALU.subtract))

                hold(pool, s_pe, G0[s] + b * GROUPS[s] + GROUPS[s] - (4 if s == RBF else 0))
                if not isinstance(kP, int) or kP > 0:
                    hold(pool, s_rec, 16 * (R0[s] + b * STORES[s]))
                K, Q, X, Y = (proj[:, i] for i in range(4))
                if s == RBF:
                    step(pool.tensor_tensor(work[:, 0], K, K, ALU.mult))
                    step(pool.tensor_tensor(work[:, 1], Q, Q, ALU.mult))
                if s == REL:
                    for i in range(2):
                        step(pool.tensor_tensor(work[:, 0], X, tables[:, 2 * i], ALU.mult))
                        step(pool.tensor_tensor(work[:, 1], Y, tables[:, 2 * i + 1], ALU.mult))
                        step(pool.tensor_tensor(work[:, 0], work[:, 0], work[:, 1], ALU.add))
                        split(work[:, 0], parts[:, 2 + i], work[:, 1])
                if s == ROPE:
                    hold(pool, s_tab, 32)
                    for z, zp in ((Q, X), (K, Y)):
                        step(pool.tensor_tensor(work[:, 0], z, tables[:, 0], ALU.mult))
                        step(pool.tensor_tensor(work[:, 1], zp, tables[:, 1], ALU.mult))
                        step(pool.tensor_tensor(z, work[:, 0], work[:, 1], ALU.add))
                rest = work if s != RBF else proj[:, 2:4]
                split(K, parts[:, 0], rest[:, 0])
                split(Q, parts[:, 1], rest[:, 1])
                if s == RBF:
                    hold(pool, s_pe, G0[s] + b * GROUPS[s] + GROUPS[s])
                    for m in range(2):
                        split(norms[:, m], nparts[:, m], norms[:, 2])
                if s != REL:
                    step(pool.tensor_tensor(values[:, par], values[:, par], wide(bv[:, s]), ALU.add))
                pool.memset(pool_flag[:, :], 0.0).then_inc(s_va, 1)
                assert n[0] == POOLOPS[s], (s, n[0])

            hold(pool, s_c, NCONST[0])
            hold(pool, s_dv, SETUP_DVE)
            hold(pool, s_x, 16 * B)
            start(0, 0, 0, 0)
            for s in range(STAGES):
                with pool.Fori(0, B) as b:
                    if s > 0:
                        with pool.If(b < B - 1):
                            finish(s - 1, (b + 1) % B, 4 * s + b - 3)
                    with pool.If(b == B - 1):
                        finish(s, 0, 4 * s)
                    with pool.If(b < B - 1):
                        start(s, (b + 1) % B, 4 * s + b + 1, (b + 1) % 2)
                    if s + 1 < STAGES:
                        with pool.If(b == B - 1):
                            start(s + 1, 0, 4 * s + 4, 0)
                    pool.nop()
            for b in range(1, B):
                finish(STAGES - 1, b, 4 * (STAGES - 1) + b)


def bf16_bits(v):
    u = np.ascontiguousarray(v, np.float32).view(np.uint32)
    return ((u + 0x7FFF + ((u >> 16) & 1)) >> 16).astype(np.uint16)


def bf16_parts(v):
    out, rest = [], np.array(v, np.float32)
    for _ in range(3):
        bits = bf16_bits(rest)
        out.append(bits)
        rest = rest - (bits.astype(np.uint32) << 16).view(np.float32)
    return out


def shape_constants():
    f = np.float32
    freq = f(1.0) / np.power(f(10000.0), np.arange(D // 2, dtype=f) / f(D // 2))
    pos = np.arange(2 * T, dtype=f)
    ang = (pos[:, None] * freq[None, :]).astype(np.float64)
    sin, cos = np.sin(ang).T, np.cos(ang).T
    own_sin = np.concatenate([sin, sin])
    swap_cos = np.concatenate([cos, -cos])

    def every_head(rows):
        return np.tile(rows, (H, 1)).astype(f)

    tables = np.stack([every_head(own_sin[:, :T]), every_head(swap_cos[:, :T]),
                       every_head(own_sin[:, T:]), every_head(swap_cos[:, T:]),
                       every_head(np.concatenate([cos, cos])[:, :T]), every_head(np.concatenate([-sin, sin])[:, :T])])
    key_parts = bf16_parts(np.concatenate([cos[:, :T], sin[:, :T]]).astype(f))
    i = np.arange(P)
    wide = np.arange(P + 1)
    return {
        "tables": tables,
        "rel_rows": np.concatenate([key_parts[p] for p in KPARTS6]),
        "ones3": bf16_bits(np.ones((3, T), f)),
        "minus3": bf16_bits(-np.ones((3, T), f)),
        "rank": np.arange(NOPS, 0, -1).astype(f),
        "ident": np.eye(P, dtype=f),
        "ident_bf": bf16_bits(np.eye(P, dtype=f)),
        "ident_int": np.eye(P, dtype=np.uint16),
        "hide_qk": bf16_bits(np.where(i[None, :] < i[:, None], f(BIG), f(0))),
        "hide_kq": bf16_bits(np.where(i[:, None] < i[None, :], f(BIG), f(0))),
        "up_qk": (i[None, :] >= i[:, None] + 2).astype(np.uint16),
        "zero_qk": (wide[None, :] == i[:, None] + 1).astype(np.uint16),
        "up_kq": (i[:, None] >= i[None, :] + 2).astype(np.uint16),
        "neghalf": np.where(i[:, None] // D == np.arange(H)[None, :], f(-0.5), f(0)).astype(f),
    }


def swap_halves(v):
    w = v.reshape(*v.shape[:-1], -1, 2, D // 2)
    return np.ascontiguousarray(w[..., ::-1, :]).reshape(v.shape)


INPUTS = ["L0_attn_a_x", "L0_attn_a_Wqkv", "L0_attn_a_bqkv", "L0_attn_a_Wo", "L0_attn_a_bo", "L0_attn_b_Wqkv",
          "L0_attn_b_bqkv", "L0_attn_b_r_sigma", "L0_attn_b_Wproj", "L0_attn_b_bproj", "L0_ffn_W", "L0_ffn_b",
          "L0_ffn_logits", "L0_ffn_u", "L1_attn_a_Wq", "L1_attn_a_Wk", "L1_attn_a_Wv", "L1_attn_a_u", "L1_attn_a_v",
          "L1_attn_a_Wo", "L1_attn_a_bo", "L1_attn_b_Wq", "L1_attn_b_bq", "L1_attn_b_Wk", "L1_attn_b_bk",
          "L1_attn_b_Wv", "L1_attn_b_bv", "L1_attn_b_Wo", "L1_attn_b_bo"]


def kernel(**inputs):
    import concourse.bacc as bacc
    from concourse.bass_utils import run_bass_kernel_spmd

    nc = bacc.Bacc("TRN2", target_bir_lowering=False, num_devices=1)
    a = {n: np.ascontiguousarray(inputs[n]) for n in INPUTS}
    a["L0_attn_b_r_sigma"] = a["L0_attn_b_r_sigma"].reshape(1, 1)
    k = shape_constants()
    k["Wq_a_swapped"] = swap_halves(np.asarray(inputs["L1_attn_a_Wq"]))
    k["v_swapped"] = swap_halves(np.asarray(inputs["L1_attn_a_v"]))
    k["Wq_b_swapped"] = swap_halves(np.asarray(inputs["L1_attn_b_Wq"]))
    k["Wk_b_swapped"] = swap_halves(np.asarray(inputs["L1_attn_b_Wk"]))
    k["bq_swapped"] = swap_halves(np.asarray(inputs["L1_attn_b_bq"]))
    k["bk_swapped"] = swap_halves(np.asarray(inputs["L1_attn_b_bk"]))
    k["ffn_weight_T"] = np.ascontiguousarray(np.asarray(inputs["L1_ffn_weight"]).T)
    disha = np.asarray(inputs["L1_ffn_disha"])
    k["disha_twice"] = np.concatenate([disha, disha])
    arrays, aps = {}, {}
    for n, v in {**a, **k}.items():
        arrays[f"in_{n}"] = v
        aps[n] = nc.dram_tensor(f"in_{n}", v.shape, mybir.dt.from_np(v.dtype), kind="ExternalInput").ap()
    out = nc.dram_tensor("out_x", (B, T, C), F32, kind="ExternalOutput").ap()
    build(nc, aps, aps, out)
    r = run_bass_kernel_spmd(nc, [arrays], core_ids=[0])
    return r.results[0]["out_x"]
```

```python
from contextlib import ExitStack

import numpy as np

import concourse.bass as bass
from concourse import mybir

F32 = mybir.dt.float32
BF16 = mybir.dt.bfloat16
U16 = mybir.dt.uint16
ALU = mybir.AluOpType
ACT = mybir.ActivationFunctionType
AX = mybir.AxisListType

B, T, C, H, D = 4, 1024, 128, 16, 8
P = 128
NT = T // P
HALF = 512
TURN = 4
TURNS = H // TURN
STAGES = 4
MASKED, RBF, REL, ROPE = range(STAGES)
EPS = 1e-5
SCALE = float(np.float32(1.0) / np.sqrt(np.float32(D)))
NOPS = 8
BIG = -1e30

BASE = 9 * D
RELROWS = 6 * D
QPARTS6, KPARTS6 = (0, 0, 1, 0, 2, 1), (0, 1, 0, 2, 0, 1)
MAXROW = [BASE, None, BASE + RELROWS, BASE]
SROWS = [BASE, None, BASE + RELROWS, BASE]
STROWS = [BASE + 3, BASE + 6, BASE + RELROWS + 3, BASE + 3]
REC = BASE + RELROWS
NLOAD = [2, 3, 5, 2]
NMAXD = [1, 0, 3, 1]


def halves(s, qt):
    lo = qt * P if s == MASKED else 0
    return [(h, max(lo, h * HALF), (h + 1) * HALF) for h in range(2) if lo < (h + 1) * HALF]


def queries(s, kt):
    return (kt + 1) * P if s == MASKED else T


FIRST = [(0, qt) for qt in range(8)] + [(1, qt) for qt in range(4)]
def banks(s, qt):
    return len(halves(s, qt)) + (s == REL)


FILL = [sum(banks(s, qt) for _, qt in FIRST) + 1 for s in range(STAGES)]
PERHEAD = [sum(banks(s, qt) for qt in range(8)) + 1 for s in range(STAGES)]
PERTURN = [TURN * n for n in PERHEAD]
SOFT = [s != RBF for s in range(STAGES)]
NTURN = B * TURNS


def before(per_stage):
    out, n = [], 0
    for x in per_stage:
        out.append(n)
        n += x
    return out


S0 = before([(FILL[s] + NTURN * PERTURN[s]) * SOFT[s] for s in range(STAGES)])
M0 = before([(1 + B * H) * SOFT[s] for s in range(STAGES)])
W0 = [s * B * H * NT for s in range(STAGES)]


def ahead(j, i):
    return ((j + 1) % TURN, 4 + i) if i < 4 else ((j + 2) % TURN, i - 4)


TO_MAX = [sum(banks(s, ahead(0, i)[1]) for i in range(6)) + 1 for s in range(STAGES)]
FIRST_TO_MAX = [sum(banks(s, qt) for qt in range(8)) + 1 for s in range(STAGES)]
GROUPS = [6, 10, 8, 10]
G0 = before([B * n for n in GROUPS])
POOLOPS = [8 + 1, 8 + 1 + 2 + 8, 16 + 6, 8 + 6 + 1]
PL0 = before([B * n for n in POOLOPS])
STORES = [18, 18 + 6, 9 + 9 + 6 + 6, 18]
R0 = before([B * n for n in STORES])
SETUP_DVE = 15 + 2 * NOPS + 2
KC = [16 * TURN * n for n in (1, 2, 2, 1)]
AHEAD_ST, AHEAD_EXP, AHEAD_PV, AHEAD_MAX, AHEAD_EV, AHEAD_OUT = 16, 2, 4, 2, 1, 16


def loads_before(s, slot):
    return 16 * sum(NLOAD[r] * (NTURN + (slot < 2)) for r in range(s))


def maxes_before(s, slot):
    return 16 * sum(NMAXD[r] * (NTURN + (slot < 1)) for r in range(s))


def build(nc, a, k, out):
    records_k = nc.dram_tensor("records_k", [2 * H, REC, T], BF16, kind="Internal").ap()
    records_q = nc.dram_tensor("records_q", [2 * H, REC, T], BF16, kind="Internal").ap()
    records_h = nc.dram_tensor("records_h", [2 * H, RELROWS, T], BF16, kind="Internal").ap()
    heads_out = nc.dram_tensor("heads_out", [B * H, P, 2 * P], F32, kind="Internal").ap()

    ctx = ExitStack()
    with ctx:
        def sb(name, shape, dt=F32):
            return ctx.enter_context(nc.sbuf_tensor(name, shape, dt))

        def ps(name, shape):
            return ctx.enter_context(nc.psum_tensor(name, shape, F32))

        def sem(name):
            return ctx.enter_context(nc.semaphore(name))

        x = sb("x", [P, B, NT, C])
        kst = [sb(f"kst{i}", [P, TURN, T], BF16) for i in range(2)]
        qst = [sb(f"qst{i}", [P, TURN, T], BF16) for i in range(2)]
        qst_up = sb("qst_up", [P, TURN, T], BF16)
        qst_zero = sb("qst_zero", [P, TURN, T], BF16)
        probs = sb("probs", [P, 4, T])
        probs_x = sb("probs_x", [P, 4, 2 * P])
        vst = sb("vst", [P, TURN, NT, 32])
        values = sb("values", [P, 2, NT, C])
        osb = sb("osb", [P, TURN, 2 * P])
        oT = sb("oT", [P, T])
        den = sb("den", [P, T])
        xn = sb("xn", [P, NT, C])
        xnT = sb("xnT", [P, T])
        proj = sb("proj", [P, 4, T])
        work = sb("work", [P, 2, T])
        parts = sb("parts", [P, 4, 3, T], BF16)
        norms = parts[0:H, 2:4].rearrange("h a p t -> h (a p t)").bitcast(F32).rearrange("h (a t) -> h a t", a=3)
        nparts = proj[0:H, 1:4].rearrange("h a t -> h (a t)").bitcast(BF16).rearrange("h (m i t) -> h m i t", m=2, i=3)
        pool_flag = sb("pool_flag", [1, 2])
        tables = sb("tables", [P, 4, T])
        stats = sb("stats", [P, NT, 6])
        meanvar = sb("meanvar", [P, NT, 2])
        rstd = sb("rstd", [P, 2, NT])
        half_pow = sb("half_pow", [P, NT])
        mx = sb("mx", [P, TURN, 3 * NT])
        mfull = sb("mfull", [P, 3, NT])
        mparts = sb("mparts", [P, 3, NT], BF16)
        mrow = sb("mrow", [3 * NT, P], BF16)
        wq = sb("wq", [P, STAGES, C])
        wqp = sb("wqp", [P, 2, C])
        wk = sb("wk", [P, STAGES, C])
        wkp = sb("wkp", [P, C])
        wv = sb("wv", [P, STAGES, C])
        wo = sb("wo", [P, STAGES, C])
        wf = sb("wf", [P, 2, C])
        wcand, bcand = (probs[:, i].rearrange("p (e c) -> p e c", e=NOPS) for i in range(2))
        bff = sb("bff", [P, C])
        wadd = sb("wadd", [P, C])
        bo = sb("bo", [P, STAGES, C])
        bv = sb("bv", [P, STAGES, C])
        cols = sb("cols", [P, 16])
        pick = sb("pick", [P, 12, NOPS])
        sig2 = sb("sig2", [P, 2])
        ident = sb("ident", [P, P])
        identb = sb("identb", [P, P], BF16)
        hide_qk = sb("hide_qk", [P, P], BF16)
        hide_kq = sb("hide_kq", [P, P], BF16)
        low_qk = sb("low_qk", [P, P + 1], BF16)
        low_kq = sb("low_kq", [P, P + 1], BF16)
        up_qk = sb("up_qk", [P, P], BF16)
        up_kq = sb("up_kq", [P, P], BF16)
        off_diag = sb("off_diag", [P, P], BF16)
        neghalf = sb("neghalf", [P, H])

        pst = ps("pst", [P, 2, T])
        pmax = ps("pmax", [P, 2, HALF])
        ppv = ps("ppv", [P, HALF])
        pm = ps("pm", [P, HALF])

        s_c = sem("s_c")
        s_kc = [sem(f"s_kc{i}") for i in range(STAGES)]
        s_ld = [sem(f"s_ld{i}") for i in range(TURN)]
        s_ldm = [sem(f"s_ldm{i}") for i in range(TURN)]
        s_st = sem("s_st")
        s_exp = sem("s_exp")
        s_pv = sem("s_pv")
        s_ev = sem("s_ev")
        s_os = [sem(f"s_os{i}") for i in range(TURN)]
        s_vs = sem("s_vs")
        s_s = sem("s_s")
        s_sm = sem("s_sm")
        s_mc = sem("s_mc")
        s_eld = sem("s_eld")
        s_rc = sem("s_rc")
        s_at = sem("s_at")
        s_xb = sem("s_xb")
        s_ep = sem("s_ep")
        s_ex = sem("s_ex")
        ln = {w: {n: sem(f"s_{w}_{n}") for n in ("stat", "aggr", "eps", "rstd", "xn", "tp", "xt")} for w in "fa"}
        s_fb = sem("s_fb")
        s_fp = sem("s_fp")
        s_fx = sem("s_fx")
        s_pp = sem("s_pp")
        s_pe = sem("s_pe")
        s_va = sem("s_va")
        s_pl = sem("s_pl")
        s_rec = sem("s_rec")
        s_tab = sem("s_tab")
        s_x = sem("s_x")
        s_top = sem("s_top")
        s_dv = sem("s_dv")
        s_ac = sem("s_ac")
        s_held = sem("s_held")
        s_fin = sem("s_fin")

        def soft_heads(s):
            return kst[s % 2], qst[s % 2]

        block = ctx.enter_context(nc.Block())

        def hold(eng, q, value):
            eng.wait_ge(q, value)
            if not isinstance(value, int):
                eng.sem_inc(s_held, 1)

        NCONST = [0]

        @block.sync
        def _(sp):
            def const(dst, src):
                sp.dma_start(dst, src).then_inc(s_c, 16)
                NCONST[0] += 16

            for b in range(B):
                sp.dma_start(x[:, b], a["L0_attn_a_x"][b].rearrange("(t p) c -> p t c", p=P)).then_inc(s_x, 16)

            def rowb(v, n=P):
                return v.rearrange("(o c) -> o c", o=1).to_broadcast([n, v.shape[0]])

            for s, (w, bias) in enumerate((("L0_attn_a_Wqkv", "L0_attn_a_bqkv"), ("L0_attn_b_Wqkv", "L0_attn_b_bqkv"))):
                for n, t in enumerate((wq, wk, wv)):
                    const(t[:, s], a[w][:, n * C:(n + 1) * C])
                const(cols[:, 2 * s:2 * s + 1], a[bias][0:C].rearrange("(c o) -> c o", o=1))
                const(cols[:, 2 * s + 1:2 * s + 2], a[bias][C:2 * C].rearrange("(c o) -> c o", o=1))
                const(bv[:, s], rowb(a[bias][2 * C:3 * C]))
            for s, n in ((2, "L1_attn_a"), (3, "L1_attn_b")):
                const(wq[:, s], a[n + "_Wq"])
                const(wk[:, s], a[n + "_Wk"])
                const(wv[:, s], a[n + "_Wv"])
            const(wqp[:, 0], k["Wq_a_swapped"])
            const(wqp[:, 1], k["Wq_b_swapped"])
            const(wkp[:, :], k["Wk_b_swapped"])
            for n, v in ((4, a["L1_attn_a_u"]), (5, a["L1_attn_a_v"]), (6, k["v_swapped"])):
                const(cols[:, n:n + 1], v.rearrange("h (d o) -> (h d) o", o=1))
            for n, v in ((7, a["L1_attn_b_bq"]), (8, a["L1_attn_b_bk"]), (9, k["bq_swapped"]), (10, k["bk_swapped"])):
                const(cols[:, n:n + 1], v.rearrange("(c o) -> c o", o=1))
            const(bv[:, 3], rowb(a["L1_attn_b_bv"]))
            for s, (w, bias) in enumerate((("L0_attn_a_Wo", "L0_attn_a_bo"), ("L0_attn_b_Wproj", "L0_attn_b_bproj"),
                                           ("L1_attn_a_Wo", "L1_attn_a_bo"), ("L1_attn_b_Wo", "L1_attn_b_bo"))):
                const(wo[:, s], a[w])
                const(bo[:, s], rowb(a[bias]))
            const(wcand, a["L0_ffn_W"].rearrange("e c n -> c e n"))
            const(bcand, a["L0_ffn_b"].rearrange("(o e) n -> o e n", o=1).to_broadcast([P, NOPS, C]))
            const(pick[:, 0], rowb(a["L0_ffn_logits"]))
            const(pick[:, 1], rowb(a["L0_ffn_u"]))
            const(pick[:, 2], rowb(k["rank"]))
            const(wf[:, 1], k["ffn_weight_T"])
            const(wadd[:, :], k["disha_twice"])
            const(sig2[:, 0:1], a["L0_attn_b_r_sigma"].to_broadcast([P, 1]))
            const(ident[:, :], k["ident"])
            const(neghalf[:, :], k["neghalf"])
            for dst, n in ((identb, "ident_bf"), (hide_qk, "hide_qk"), (hide_kq, "hide_kq"), (low_qk, "low_qk"),
                           (low_kq, "low_kq"), (up_qk, "up_qk"), (up_kq, "up_kq"), (off_diag, "off_diag")):
                const(dst[:, :], k[n].bitcast(BF16))
            for n in range(4):
                const(tables[:, n], k["tables"][n])

            def const_rows(s):
                keys, qs = soft_heads(s)
                r = MAXROW[s]
                for slot in range(TURN):
                    if s == RBF:
                        sp.dma_start(keys[BASE + 3:BASE + 6, slot], k["ones3"].bitcast(BF16)).then_inc(s_kc[s], 16)
                        sp.dma_start(qs[BASE:BASE + 3, slot], k["ones3"].bitcast(BF16)).then_inc(s_kc[s], 16)
                    else:
                        sp.dma_start(keys[r:r + 3, slot], k["minus3"].bitcast(BF16)).then_inc(s_kc[s], 16)
                    if s == REL:
                        sp.dma_start(keys[BASE:REC, slot], k["rel_rows"].bitcast(BF16)).then_inc(s_kc[s], 16)

            def load(s, slot, rec):
                keys, qs = soft_heads(s)
                if s == RBF:
                    pairs = [(keys[0:BASE + 3, slot], records_k[rec, 0:BASE + 3]),
                             (qs[0:BASE, slot], records_q[rec, 0:BASE]),
                             (qs[BASE + 3:BASE + 6, slot], records_q[rec, BASE:BASE + 3])]
                elif s == REL:
                    pairs = [(keys[0:BASE, slot], records_k[rec, 0:BASE]),
                             (qs[0:REC, slot], records_q[rec, 0:REC]),
                             (qst_up[0:BASE, slot], records_q[rec, 0:BASE]),
                             (qst_up[BASE:REC, slot, 0:T - 1], records_h[rec, :, 1:T]),
                             (qst_zero[0:BASE, slot], records_q[rec, 0:BASE])]
                else:
                    pairs = [(keys[0:BASE, slot], records_k[rec, 0:BASE]), (qs[0:BASE, slot], records_q[rec, 0:BASE])]
                for dst, src in pairs:
                    sp.dma_start(dst, src).then_inc(s_ld[slot], 16)

            def place_max(s, slot, count):
                sp.wait_ge(s_sm, count + AHEAD_MAX)
                r = MAXROW[s]
                for dst in ([qst[s % 2]] if s != REL else [qst[0], qst_up, qst_zero]):
                    sp.dma_start(dst[r:r + 3, slot], mrow[:, :]).then_inc(s_ldm[slot], 16)

            def store_records(s, b, par):
                done = PL0[s] + b * POOLOPS[s]
                lo = par * H
                def rows(t, r, src):
                    sp.dma_start(t[bass.ds(lo, H), r:r + D], src).then_inc(s_rec, 16)
                sp.wait_ge(s_pl, done + POOLOPS[s])
                for i in range(3):
                    for j in range(3):
                        rows(records_k, (3 * i + j) * D, parts[:, 0, j])
                        rows(records_q, (3 * i + j) * D, parts[:, 1, i])
                if s == REL:
                    for i, p in enumerate(QPARTS6):
                        rows(records_q, BASE + i * D, parts[:, 2, p])
                        rows(records_h, i * D, parts[:, 3, p])
                if s == RBF:
                    for i in range(3):
                        sp.dma_start(records_k[bass.ds(lo, H), BASE + i], nparts[:, 0, i]).then_inc(s_rec, 16)
                        sp.dma_start(records_q[bass.ds(lo, H), BASE + i], nparts[:, 1, i]).then_inc(s_rec, 16)

            def load_outputs(s, b, kE):
                if not isinstance(kE, int) or kE > 0:
                    sp.wait_ge(s_ep, 2 * kE)
                for j in range(TURN):
                    sp.wait_ge(s_os[j], 16 * (NTURN * s + TURNS * b + TURNS) + AHEAD_OUT)
                o = heads_out[bass.ds(b * H, H)]
                for g in range(4):
                    q = slice(g * 2 * P, (g + 1) * 2 * P)
                    sp.dma_start(oT[:, q], o[:, 32 * g:32 * g + D]).then_inc(s_eld, 16)
                    sp.dma_start(den[:, q], o[:, 32 * g + D:32 * g + D + 1].to_broadcast([H, D, 2 * P])).then_inc(s_eld, 16)

            const_rows(0)
            for s in range(STAGES):
                if s == 0:
                    store_records(0, 0, 0)
                sp.wait_ge(s_rec, 16 * (R0[s] + STORES[s]))
                if s + 1 < STAGES:
                    if s + 1 >= 2:
                        sp.wait_ge(s_st, W0[s] + AHEAD_ST)
                        for n in range(2):
                            sp.wait_ge(s_ld[n], loads_before(s, n))
                        if SOFT[s - 1]:
                            sp.wait_ge(s_ldm[0], maxes_before(s, 0))
                    const_rows(s + 1)
                for n in range(2):
                    sp.wait_ge(s_st, W0[s] + AHEAD_ST)
                    load(s, n, n)
                if SOFT[s]:
                    place_max(s, 0, S0[s] + FIRST_TO_MAX[s])
                with sp.Fori(0, B) as b, sp.Fori(0, TURNS) as c:
                    g = b * TURNS + c
                    if s > 0:
                        with sp.If(c == 0):
                            with sp.If(b < B - 1):
                                load_outputs(s - 1, (b + 1) % B, 4 * s + b - 3)
                    with sp.If(c == 0):
                        with sp.If(b == B - 1):
                            load_outputs(s, 0, 4 * s)
                    if s == REL:
                        with sp.If(g == NTURN - TURNS):
                            sp.wait_ge(s_pl, PL0[ROPE])
                            for n in range(2):
                                sp.dma_start(tables[:, n], k["tables"][4 + n]).then_inc(s_tab, 16)
                    for j in range(TURN):
                        if j == 1:
                            with sp.If(c == TURNS - 1):
                                with sp.If(b < B - 1):
                                    store_records(s, (b + 1) % B, (b + 1) % 2)
                                if s + 1 < STAGES:
                                    with sp.If(b == B - 1):
                                        store_records(s + 1, 0, 0)
                        if j == 2:
                            with sp.If(c == TURNS - 1):
                                with sp.If(b < B - 1):
                                    hold(sp, s_rec, 16 * (R0[s] + (b + 2) * STORES[s]))
                                if s + 1 < STAGES:
                                    with sp.If(b == B - 1):
                                        sp.wait_ge(s_rec, 16 * (R0[s + 1] + STORES[s + 1]))
                        sp.wait_ge(s_st, W0[s] + NT * (TURN * g + j - 1) + AHEAD_ST)
                        load(s, (j + 2) % TURN, (g * TURN + (j + 2)) % (2 * H))
                        if j:
                            sp.wait_ge(s_ev, B * H * s + TURN * g + j + AHEAD_EV)
                            sp.dma_start(heads_out[g * TURN + (j - 1)], osb[:, j - 1]).then_inc(s_os[j - 1], 16)
                        if SOFT[s]:
                            place_max(s, (j + 1) % TURN, S0[s] + FILL[s] + g * PERTURN[s] + (j * PERHEAD[s] + TO_MAX[s]))
                    sp.wait_ge(s_ev, B * H * s + TURN * g + TURN + AHEAD_EV)
                    sp.dma_start(heads_out[g * TURN + (TURN - 1)], osb[:, TURN - 1]).then_inc(s_os[TURN - 1], 16)
            for b in range(1, B):
                load_outputs(STAGES - 1, b, 4 * (STAGES - 1) + b)
            for b in range(B):
                sp.wait_ge(s_fx, 2 * (4 * (STAGES - 1) + b + 1))
                sp.dma_start(out[b].rearrange("(t p) c -> p t c", p=P), x[:, b]).then_inc(s_fin, 16)
            sp.wait_ge(s_fin, 16 * B)
            for n in range(2):
                sp.wait_ge(s_ld[n], loads_before(STAGES, n))
            sp.wait_ge(s_ldm[0], maxes_before(STAGES, 0))

        @block.tensor
        def _(pe):
            def scores_qk(s, slot, qt, v, n, odd):
                keys, qs = soft_heads(s)
                R = SROWS[s]
                q = slice(qt * P, (qt + 1) * P)
                for h, lo, hi in halves(s, qt):
                    pe.wait_ge(s_sm, v + (n + 1))
                    bank = pmax[:, (n + odd) % 2]
                    if s == REL:
                        cut = min(max((qt + 1) * P, lo), hi)
                        m0, m1 = max(qt * P, lo), min((qt + 1) * P + 1, hi)
                        for qq, p0, p1 in ((qst[0], lo, cut), (qst_up, cut, hi)):
                            if p1 > p0:
                                mm = pe.matmul(bank[:, p0 - h * HALF:p1 - h * HALF], qq[0:R, slot, q],
                                               keys[0:R, slot, p0:p1], start=p0 == lo, stop=p1 == hi and m1 <= m0)
                        if m1 > m0:
                            mm = pe.matmul(bank[:, m0 - h * HALF:m1 - h * HALF], identb[:, :],
                                           low_qk[:, m0 - qt * P:m1 - qt * P], start=False, stop=True)
                    else:
                        diag = s == MASKED and lo == qt * P
                        mm = pe.matmul(bank[:, lo - h * HALF:hi - h * HALF], qs[0:R, slot, q], keys[0:R, slot, lo:hi],
                                       start=True, stop=not diag)
                        if diag:
                            mm = pe.matmul(bank[:, lo - h * HALF:lo - h * HALF + P], identb[:, :], hide_qk[:, :],
                                           start=False, stop=True)
                    mm.then_inc(s_s, 1)
                    n += 1
                return n

            def alternatives_qk(s, slot, qt, v, n, odd):
                keys, qs = soft_heads(s)
                R = SROWS[s]
                q = slice(qt * P, (qt + 1) * P)
                if s == REL:
                    pe.wait_ge(s_sm, v + (n + 1))
                    bank = pmax[:, (n + odd) % 2]
                    m = P if qt < NT - 1 else P - 1
                    pe.matmul(bank[:, 0:P], qst_up[0:R, slot, q], keys[0:R, slot, q], start=True, stop=False)
                    pe.matmul(bank[:, 0:P], identb[:, :], up_qk[:, :], start=False, stop=False)
                    pe.matmul(bank[:, P:P + m], qs[0:BASE, slot, q], keys[0:BASE, slot, qt * P + 1:qt * P + 1 + m],
                              start=False, stop=False)
                    pe.matmul(bank[:, P:P + m], identb[:, :], off_diag[:, 0:m], start=False, stop=True).then_inc(s_s, 1)
                    n += 1
                return n

            def scores_kq(s, slot, kt, w):
                keys, qs = soft_heads(s)
                R = STROWS[s]
                kk = keys[0:R, slot, kt * P:(kt + 1) * P]
                buf = pst[:, kt % 2]
                pe.wait_ge(s_exp, w - 1 + AHEAD_EXP)
                nq = queries(s, kt)
                for lo in range(0, nq, HALF):
                    hi = min(lo + HALF, nq)
                    if s == REL:
                        cut = min(max(kt * P, lo), hi)
                        first = kt * P - 1
                        m0, m1 = max(first, lo), min((kt + 1) * P, hi)
                        for qq, p0, p1 in ((qst_up, lo, cut), (qst[0], cut, hi)):
                            if p1 > p0:
                                mm = pe.matmul(buf[:, p0:p1], kk, qq[0:R, slot, p0:p1], start=p0 == lo,
                                               stop=p1 == hi and m1 <= m0)
                        if m1 > m0:
                            mm = pe.matmul(buf[:, m0:m1], identb[:, :], low_kq[:, m0 - first:m1 - first],
                                           start=False, stop=True)
                    else:
                        diag = s == MASKED and hi == nq
                        mm = pe.matmul(buf[:, lo:hi], kk, qs[0:R, slot, lo:hi], start=True, stop=not diag)
                        if diag:
                            mm = pe.matmul(buf[:, nq - P:nq], identb[:, :], hide_kq[:, :], start=False, stop=True)
                if s == REL:
                    pe.wait_ge(s_exp, w + AHEAD_EXP)
                    c = 1 if kt == 0 else 0
                    alt = pm[:, 2 * P:4 * P]
                    pe.matmul(alt[:, c:P], kk, qst_zero[0:R, slot, kt * P - 1 + c:(kt + 1) * P - 1], start=True, stop=False)
                    pe.matmul(alt[:, c:P], identb[:, :], off_diag[:, c:P], start=False, stop=False)
                    pe.matmul(alt[:, P:2 * P], kk, qst_up[0:R, slot, kt * P:(kt + 1) * P], start=False, stop=False)
                    mm = pe.matmul(alt[:, P:2 * P], identb[:, :], up_kq[:, :], start=False, stop=True)
                mm.then_inc(s_st, 1)

            def pv(s, j, i, w, N):
                kt = NT - 1 - i
                pe.wait_ge(s_exp, w + 1 + AHEAD_EXP)
                if i == 0:
                    pe.wait_ge(s_ev, N + AHEAD_EV)
                    pe.wait_ge(s_vs, N + 1)
                nq = queries(s, kt)

                def alternatives():
                    first = kt * P
                    spans = [(first, P, 2 * P), (first, 1, P)] + ([(first - 1, 0, 1)] if kt else [])
                    for q, c0, c1 in spans:
                        g, at = q // (2 * P), q % (2 * P)
                        pe.matmul(ppv[32 * g:32 * g + 32, at:at + c1 - c0], vst[:, j, kt, :], probs_x[:, i % 4, c0:c1],
                                  start=False, stop=False, tile_position=(0, 32 * g))

                if s == REL and i > 0:
                    alternatives()
                for g in range(4):
                    n = min(2 * P, nq - g * 2 * P)
                    if n <= 0:
                        continue
                    last = max(0, 2 * g) if s == MASKED else 0
                    mm = pe.matmul(ppv[32 * g:32 * g + 32, 0:n], vst[:, j, kt, :],
                                   probs[:, i % 4, g * 2 * P:g * 2 * P + n],
                                   start=(i == 0), stop=(kt == last), tile_position=(0, 32 * g))
                if s == REL and i == 0:
                    alternatives()
                mm.then_inc(s_pv, 1)

            def turn_max(count, v, n, odd):
                pe.wait_ge(s_mc, 6 * count)
                pe.wait_ge(s_sm, v + (n + 1))
                pe.transpose(pmax[:, (n + odd) % 2].bitcast(BF16)[0:3 * NT, 0:P], mparts[:, :, :].rearrange("p a t -> p (a t)"),
                             identb[:, :]).then_inc(s_s, 1)
                return n + 1

            def layer_norm(w, n):
                for h in range(2):
                    if h == 0:
                        pe.wait_ge(ln[w]["xn"], NT * (n + 1))
                    else:
                        pe.wait_ge(ln[w]["xt"], 2 * n + 1)
                    for t in range(4):
                        mm = pe.transpose(pm[:, t * P:(t + 1) * P], xn[:, 4 * h + t], ident[:, :])
                    mm.then_inc(ln[w]["tp"], 1)
                pe.wait_ge(ln[w]["xt"], 2 * n + 2)

            def finish(s, b, kE):
                pe.wait_ge(s_eld, 128 * (kE + 1))
                if SOFT[s]:
                    pe.wait_ge(s_at, 4 * sum(SOFT[:s]) + b + 1)
                for h in range(2):
                    if h:
                        pe.wait_ge(s_ex, 2 * kE + 1)
                    for t in range(4):
                        mm = pe.matmul(pm[:, t * P:(t + 1) * P], oT[:, (4 * h + t) * P:(4 * h + t + 1) * P], wo[:, s],
                                       start=True, stop=True)
                    mm.then_inc(s_ep, 1)
                pe.wait_ge(s_ex, 2 * kE + 2)
                layer_norm("f", kE)
                for h in range(2):
                    if h:
                        pe.wait_ge(s_fx, 2 * kE + 1)
                    for t in range(4):
                        mm = pe.matmul(pm[:, t * P:(t + 1) * P], xnT[:, (4 * h + t) * P:(4 * h + t + 1) * P], wf[:, s // 2],
                                       start=True, stop=True)
                    mm.then_inc(s_fp, 1)
                pe.wait_ge(s_fx, 2 * kE + 2)

            def start(s, b, kP):
                layer_norm("a", kP)
                n = G0[s] + b * GROUPS[s]
                ws = {0: [wq[:, 0], wk[:, 0]], 1: [wk[:, 1], wq[:, 1]], 2: [wq[:, 2], wqp[:, 0], wk[:, 2]],
                      3: [wq[:, 3], wqp[:, 1], wk[:, 3], wkp[:, :]]}[s]
                k = 0

                def bank():
                    if k > 1:
                        pe.wait_ge(s_pe, n + (k - 1))
                    return (pm, ppv)[k % 2]

                for w in ws:
                    for h in range(2):
                        pe.matmul(bank()[:, :], w, xnT[:, h * HALF:(h + 1) * HALF], start=True, stop=True).then_inc(s_pp, 1)
                        k += 1
                for h in range(2):
                    into = bank()
                    for t in range(4):
                        mm = pe.matmul(into[:, t * P:(t + 1) * P], xnT[:, (4 * h + t) * P:(4 * h + t + 1) * P], wv[:, s],
                                       start=True, stop=True)
                    mm.then_inc(s_pp, 1)
                    k += 1
                if s == RBF:
                    pe.wait_ge(s_pl, PL0[s] + b * POOLOPS[s] + 2)
                    for m in range(2):
                        for h in range(2):
                            pe.matmul(bank()[0:H, :], neghalf[:, :], work[:, m, h * HALF:(h + 1) * HALF],
                                      start=True, stop=True).then_inc(s_pp, 1)
                            k += 1
                pe.wait_ge(s_pe, n + k)

            pe.wait_ge(s_c, NCONST[0])
            pe.wait_ge(s_dv, SETUP_DVE)
            start(0, 0, 0)
            for s in range(STAGES):
                pe.wait_ge(s_kc[s], KC[s])
                v = 0
                if SOFT[s]:
                    for n, qt in FIRST:
                        if qt == 0:
                            pe.wait_ge(s_ld[n], loads_before(s, n) + 16 * NLOAD[s])
                        v = scores_qk(s, n, qt, S0[s], v, S0[s] % 2)
                        v = alternatives_qk(s, n, qt, S0[s], v, S0[s] % 2)
                        if n == 0 and qt == 7:
                            v = turn_max(M0[s] + 1, S0[s], v, S0[s] % 2)
                with pe.Fori(0, B) as b, pe.Fori(0, TURNS) as c:
                    g = b * TURNS + c
                    with pe.If(c == 1):
                        if s > 0:
                            with pe.If(b < B - 1):
                                finish(s - 1, (b + 1) % B, 4 * s + b - 3)
                        with pe.If(b == B - 1):
                            finish(s, 0, 4 * s)
                        pe.wait_ge(s_ev, B * H * s + TURN * g + AHEAD_EV)
                        with pe.If(b < B - 1):
                            start(s, (b + 1) % B, 4 * s + b + 1)
                        if s + 1 < STAGES:
                            with pe.If(b == B - 1):
                                start(s + 1, 0, 4 * s + 4)
                        pe.nop()
                    v0 = S0[s] + FILL[s] + g * PERTURN[s]
                    v = 0
                    w0 = W0[s] + g * NT * TURN
                    for j in range(TURN):
                        n = TURN * g + j
                        for i in range(NT):
                            w = w0 + NT * j + i
                            if SOFT[s]:
                                slot, qt = ahead(j, i)
                                if i == 4:
                                    pe.wait_ge(s_ld[slot], loads_before(s, slot) + 16 * NLOAD[s] * (g + (j + 2) // TURN + 1))
                                v = scores_qk(s, slot, qt, v0, v, (S0[s] + FILL[s]) % 2)
                            if i == 0:
                                if SOFT[s]:
                                    pe.wait_ge(s_ldm[j], maxes_before(s, j) + 16 * NMAXD[s] * (g + 1))
                                else:
                                    pe.wait_ge(s_ld[j], loads_before(s, j) + 16 * NLOAD[s] * (g + 1))
                            scores_kq(s, j, NT - 1 - i, w)
                            if SOFT[s]:
                                v = alternatives_qk(s, slot, qt, v0, v, (S0[s] + FILL[s]) % 2)
                            if SOFT[s] and i == 5:
                                v = turn_max(M0[s] + n + 2, v0, v, (S0[s] + FILL[s]) % 2)
                            if NT * j + i >= 2:
                                jj, ii = divmod(NT * j + i - 2, NT)
                                pv(s, jj, ii, w - 2, B * H * s + TURN * g + jj)
                    for ii in (NT - 2, NT - 1):
                        pv(s, TURN - 1, ii, w0 + NT * (TURN - 1) + ii, B * H * s + TURN * g + TURN - 1)
            for b in range(1, B):
                finish(STAGES - 1, b, 4 * (STAGES - 1) + b)

        @block.scalar
        def _(act):
            def stage_values(slot, par, h, need=None):
                nc.scalar.activation(vst[:, slot, :, 0:D], values[:, par, :, bass.ds(h * D, D)] if not isinstance(h, int)
                                     else values[:, par, :, h * D:(h + 1) * D], ACT.Copy).then_inc(s_vs, 1)

            def take_out(s, g, j):
                act.wait_ge(s_pv, W0[s] + NT * (TURN * g + j + 1) + AHEAD_PV)
                act.wait_ge(s_os[j], 16 * (NTURN * s + g) + AHEAD_OUT)
                nc.scalar.activation(osb[:, j], ppv[:, 0:2 * P], ACT.Copy).then_inc(s_ev, 1)

            def layer_norm(w, n):
                for h in range(2):
                    act.wait_ge(ln[w]["tp"], 2 * n + h + 1)
                    nc.scalar.activation(xnT[:, h * HALF:(h + 1) * HALF], pm[:, :], ACT.Copy).then_inc(ln[w]["xt"], 1)

            def start(s, b, kP, par):
                layer_norm("a", kP)
                n = G0[s] + b * GROUPS[s]
                if not isinstance(kP, int) or kP > 0:
                    act.wait_ge(s_pl, PL0[s] + b * POOLOPS[s])
                    if s in (RBF, REL):
                        act.wait_ge(s_rec, 16 * (R0[s] + b * STORES[s]))
                dst = {0: [[(1, 0)], [(0, 1)]], 1: [[(1, 3)], [(0, 2)]], 2: [[(1, 4), (2, 5)], [(3, 6)], [(0, None)]],
                       3: [[(1, 7)], [(2, 9)], [(0, 8)], [(3, 10)]]}[s]
                k = 0
                for targets in dst:
                    for h in range(2):
                        k += 1
                        act.wait_ge(s_pp, n + k)
                        bank = (ppv, pm)[k % 2]
                        for slot, col in targets:
                            o = proj[:, slot, h * HALF:(h + 1) * HALF]
                            if col is None:
                                ins = nc.scalar.activation(o, bank[:, :], ACT.Copy)
                            else:
                                ins = nc.scalar.activation(o, bank[:, :], ACT.Identity, bias=cols[:, col:col + 1])
                        ins.then_inc(s_pe, 1)
                for h in range(2):
                    k += 1
                    act.wait_ge(s_pp, n + k)
                    bank = (ppv, pm)[k % 2]
                    nc.scalar.activation(values[:, par, 4 * h:4 * h + 4], bank[:, :].rearrange("p (t c) -> p t c", t=4), ACT.Copy)\
                        .then_inc(s_pe, 1)
                if s == RBF:
                    for m in range(2):
                        for h in range(2):
                            k += 1
                            act.wait_ge(s_pp, n + k)
                            bank = (ppv, pm)[k % 2]
                            nc.scalar.activation(norms[:, m, h * HALF:(h + 1) * HALF], bank[0:H, :], ACT.Copy).then_inc(s_pe, 1)

            act.wait_ge(s_c, NCONST[0])
            nc.scalar.activation(pick[:, 4], pick[:, 1], ACT.Ln).then_inc(s_ac, 1)
            act.wait_ge(s_ac, 1)
            nc.scalar.activation(pick[:, 5], pick[:, 4], ACT.Ln, scale=-1.0).then_inc(s_ac, 1)
            act.wait_ge(s_dv, 7)
            nc.scalar.activation(pick[:, 6], pick[:, 3], ACT.Exp).then_inc(s_ac, 1)
            act.wait_ge(s_dv, 8)
            nc.scalar.activation(pick[:, 8, 0:1], pick[:, 7, 0:1], ACT.Ln).then_inc(s_ac, 1)
            start(0, 0, 0, 0)
            act.wait_ge(s_va, 1)
            for j in range(TURN):
                stage_values(j, 0, j)
            for s in range(STAGES):
                scale = sig2[:, 1:2] if s == RBF else SCALE
                with act.Fori(0, B) as b, act.Fori(0, TURNS) as c:
                    g = b * TURNS + c
                    with act.If(c == 1):
                        if s > 0:
                            with act.If(b < B - 1):
                                layer_norm("f", 4 * s + b - 3)
                        with act.If(b == B - 1):
                            layer_norm("f", 4 * s)
                        with act.If(b < B - 1):
                            start(s, (b + 1) % B, 4 * s + b + 1, (b + 1) % 2)
                        if s + 1 < STAGES:
                            with act.If(b == B - 1):
                                start(s + 1, 0, 4 * s + 4, 0)
                        act.nop()
                    with act.If(c == TURNS - 1):
                        if s + 1 < STAGES:
                            hold(act, s_va, 4 * s + b + 2)
                        else:
                            with act.If(b < B - 1):
                                hold(act, s_va, 4 * s + b + 2)
                        act.nop()
                    w0 = W0[s] + g * NT * TURN
                    nxt = (g + 1) % (2 * TURNS)
                    for j in range(TURN):
                        for i in range(NT):
                            w = w0 + NT * j + i
                            act.wait_ge(s_st, w + 1 + AHEAD_ST)
                            act.wait_ge(s_pv, w - 3 + AHEAD_PV)
                            nq = queries(s, NT - 1 - i)
                            ins = nc.scalar.activation(probs[:, i % 4, 0:nq], pst[:, (NT - 1 - i) % 2, 0:nq], ACT.Exp,
                                                       scale=scale)
                            if s == REL:
                                alt = slice(1 if i == NT - 1 else 0, 2 * P)
                                ins = nc.scalar.activation(probs_x[:, i % 4, alt], pm[:, 2 * P:4 * P][:, alt], ACT.Exp,
                                                           scale=scale)
                            ins.then_inc(s_exp, 1)
                            if j and i == 1:
                                take_out(s, g, j - 1)
                                stage_values(j - 1, nxt // TURNS, (nxt % TURNS) * TURN + (j - 1))
                    take_out(s, g, TURN - 1)
                    stage_values(TURN - 1, nxt // TURNS, (nxt % TURNS) * TURN + (TURN - 1))
            for b in range(1, B):
                layer_norm("f", 4 * (STAGES - 1) + b)

        @block.vector
        def _(dve):
            def reduce_qk(s, slot, qt, v, n, odd):
                for h, lo, hi in halves(s, qt):
                    dve.wait_ge(s_s, v + (n + 1))
                    dve.tensor_reduce(mx[:, slot, h * NT + qt:h * NT + qt + 1], pmax[:, (n + odd) % 2, lo - h * HALF:hi - h * HALF],
                                      AX.X, ALU.max).then_inc(s_sm, 1)
                    n += 1
                if s == REL:
                    m = P if qt < NT - 1 else P - 1
                    dve.wait_ge(s_s, v + (n + 1))
                    dve.tensor_reduce(mx[:, slot, 2 * NT + qt:2 * NT + qt + 1], pmax[:, (n + odd) % 2, 0:P + m],
                                      AX.X, ALU.max).then_inc(s_sm, 1)
                    n += 1
                return n

            def split_max(s, slot, count, v):
                n = 6 * (count - 1)
                third = 2 * NT if s == REL else 0
                dve.wait_ge(s_sm, v + AHEAD_MAX)
                dve.tensor_tensor(mfull[:, 2], mx[:, slot, 0:NT], mx[:, slot, NT:2 * NT], ALU.max).then_inc(s_mc, 1)
                dve.wait_ge(s_mc, n + 1)
                dve.tensor_tensor(mfull[:, 0], mfull[:, 2], mx[:, slot, third:third + NT], ALU.max).then_inc(s_mc, 1)
                dve.wait_ge(s_mc, n + 2)
                dve.tensor_copy(mparts[:, 0], mfull[:, 0]).then_inc(s_mc, 1)
                dve.wait_ge(s_mc, n + 3)
                dve.tensor_tensor(mfull[:, 1], mfull[:, 0], mparts[:, 0], ALU.subtract).then_inc(s_mc, 1)
                dve.wait_ge(s_mc, n + 4)
                dve.tensor_copy(mparts[:, 1], mfull[:, 1]).then_inc(s_mc, 1)
                dve.wait_ge(s_mc, n + 5)
                dve.tensor_tensor(mparts[:, 2], mfull[:, 1], mparts[:, 1], ALU.subtract).then_inc(s_mc, 1)

            def copy_max(slot, landed, v, n, odd):
                dve.wait_ge(s_s, v + (n + 1))
                if landed is not None:
                    dve.wait_ge(s_ldm[slot], landed)
                dve.tensor_copy(mrow[:, :], pmax[:, (n + odd) % 2].bitcast(BF16)[0:3 * NT, 0:P]).then_inc(s_sm, 1)
                return n + 1

            def layer_norm(w, n, b):
                xb = x[:, b]
                for t in range(NT):
                    dve.bn_stats(stats[:, t], xb[:, t]).then_inc(ln[w]["stat"], 1)
                hold(dve, ln[w]["stat"], NT * (n + 1))
                for t in range(NT):
                    dve.bn_aggr(meanvar[:, t], stats[:, t]).then_inc(ln[w]["aggr"], 1)
                dve.wait_ge(ln[w]["rstd"], n + 1)
                for t in range(NT):
                    dve.tensor_scalar(xn[:, t], xb[:, t], meanvar[:, t, 0:1], rstd[:, 1, t:t + 1], ALU.subtract, ALU.mult)\
                        .then_inc(ln[w]["xn"], 1)

            def finish(s, b, kE):
                xb = x[:, b]
                dve.wait_ge(s_eld, 128 * (kE + 1))
                if SOFT[s]:
                    soft = 4 * sum(SOFT[:s]) + b
                    dve.reciprocal(den[:, :], den[:, :]).then_inc(s_rc, 1)
                    dve.wait_ge(s_rc, soft + 1)
                    dve.tensor_tensor(oT[:, :], oT[:, :], den[:, :], ALU.mult).then_inc(s_at, 1)
                dve.wait_ge(s_xb, kE + 1)
                for h in range(2):
                    dve.wait_ge(s_ep, 2 * kE + h + 1)
                    dve.tensor_tensor(xb[:, 4 * h:4 * h + 4], pm[:, :].rearrange("p (t c) -> p t c", t=4),
                                      xb[:, 4 * h:4 * h + 4], ALU.add).then_inc(s_ex, 1)
                hold(dve, s_ex, 2 * kE + 2)
                layer_norm("f", kE, b)
                if s < 2:
                    dve.wait_ge(s_fb, kE + 1)
                for h in range(2):
                    dve.wait_ge(s_fp, 2 * kE + h + 1)
                    dve.tensor_tensor(xb[:, 4 * h:4 * h + 4], pm[:, :].rearrange("p (t c) -> p t c", t=4),
                                      xb[:, 4 * h:4 * h + 4], ALU.add).then_inc(s_fx, 1)

            dve.memset(vst[:, :, :, :], 0.0).then_inc(s_dv, 1)
            dve.memset(half_pow[:, :], -0.5).then_inc(s_dv, 1)
            dve.memset(mx[:, :, :], 3.0 * BIG).then_inc(s_dv, 1)
            dve.memset(qst_up[:, :, :], 0.0).then_inc(s_dv, 1)
            dve.memset(qst_zero[:, :, :], 0.0).then_inc(s_dv, 1)
            dve.wait_ge(s_dv, 5)
            dve.memset(vst[:, :, :, D:D + 1], 1.0).then_inc(s_dv, 1)
            for q, n in ((s_st, AHEAD_ST), (s_exp, AHEAD_EXP), (s_pv, AHEAD_PV), (s_sm, AHEAD_MAX), (s_ev, AHEAD_EV),
                         *((s_os[j], AHEAD_OUT) for j in range(TURN))):
                dve.sem_inc(q, n)
            dve.wait_ge(s_c, NCONST[0])
            dve.tensor_reduce(pick[:, 7, 1:2], pick[:, 0], AX.X, ALU.max).then_inc(s_top, 1)
            dve.wait_ge(s_top, 1)
            dve.tensor_scalar(pick[:, 3], pick[:, 0], pick[:, 7, 1:2], None, ALU.subtract).then_inc(s_dv, 1)
            dve.wait_ge(s_ac, 3)
            dve.tensor_reduce(pick[:, 7, 0:1], pick[:, 6], AX.X, ALU.add).then_inc(s_dv, 1)
            dve.wait_ge(s_ac, 4)
            dve.tensor_scalar(pick[:, 9], pick[:, 3], pick[:, 8, 0:1], None, ALU.subtract).then_inc(s_dv, 1)
            dve.wait_ge(s_dv, 9)
            dve.tensor_tensor(pick[:, 9], pick[:, 9], pick[:, 5], ALU.subtract).then_inc(s_dv, 1)
            dve.wait_ge(s_dv, 10)
            dve.tensor_reduce(pick[:, 10, 0:1], pick[:, 9], AX.X, ALU.max).then_inc(s_dv, 1)
            dve.wait_ge(s_dv, 11)
            dve.tensor_scalar(pick[:, 11], pick[:, 9], pick[:, 10, 0:1], None, ALU.is_equal).then_inc(s_dv, 1)
            dve.wait_ge(s_dv, 12)
            dve.tensor_tensor(pick[:, 11], pick[:, 11], pick[:, 2], ALU.mult).then_inc(s_dv, 1)
            dve.wait_ge(s_dv, 13)
            dve.tensor_reduce(pick[:, 10, 0:1], pick[:, 11], AX.X, ALU.max).then_inc(s_dv, 1)
            dve.wait_ge(s_dv, 14)
            dve.tensor_scalar(pick[:, 11], pick[:, 2], pick[:, 10, 0:1], None, ALU.is_equal).then_inc(s_dv, 1)
            dve.wait_ge(s_dv, 15)
            dve.tensor_scalar(wf[:, 0], wcand[:, 0], pick[:, 11, 0:1], None, ALU.mult).then_inc(s_dv, 1)
            dve.tensor_scalar(bff[:, :], bcand[:, 0], pick[:, 11, 0:1], None, ALU.mult).then_inc(s_dv, 1)
            for e in range(1, NOPS):
                dve.wait_ge(s_dv, 15 + 2 * e)
                for dst, src in ((wf[:, 0], wcand[:, e]), (bff[:, :], bcand[:, e])):
                    dve.scalar_tensor_tensor(out=dst, in0=src, scalar=pick[:, 11, e:e + 1], in1=dst, op0=ALU.mult,
                                             op1=ALU.add).then_inc(s_dv, 1)
            dve.tensor_tensor(wf[:, 1], wf[:, 1], wadd[:, :], ALU.add).then_inc(s_dv, 1)
            dve.tensor_scalar(sig2[:, 1:2], sig2[:, 0:1], 2.0, None, ALU.mult).then_inc(s_dv, 1)
            dve.wait_ge(s_x, 16 * B)
            layer_norm("a", 0, 0)
            for s in range(STAGES):
                v = 0
                if SOFT[s]:
                    for n, qt in FIRST:
                        v = reduce_qk(s, n, qt, S0[s], v, S0[s] % 2)
                        if n == 0 and qt == 7:
                            split_max(s, 0, M0[s] + 1, S0[s] + v)
                            v = copy_max(0, maxes_before(s, 0) or None, S0[s], v, S0[s] % 2)
                with dve.Fori(0, B) as b, dve.Fori(0, TURNS) as c:
                    g = b * TURNS + c
                    with dve.If(c == 1):
                        if s > 0:
                            with dve.If(b < B - 1):
                                finish(s - 1, (b + 1) % B, 4 * s + b - 3)
                        with dve.If(b == B - 1):
                            finish(s, 0, 4 * s)
                        with dve.If(b < B - 1):
                            if s > 0:
                                hold(dve, s_fx, 2 * (4 * s + b - 3) + 2)
                            layer_norm("a", 4 * s + b + 1, (b + 1) % B)
                        if s + 1 < STAGES:
                            with dve.If(b == B - 1):
                                dve.wait_ge(s_fx, 2 * 4 * s + 2)
                                layer_norm("a", 4 * s + 4, 0)
                        dve.nop()
                    v0 = S0[s] + FILL[s] + g * PERTURN[s]
                    v = 0
                    for j in range(TURN):
                        n = TURN * g + j
                        for i in range(NT):
                            if not SOFT[s]:
                                continue
                            slot, qt = ahead(j, i)
                            v = reduce_qk(s, slot, qt, v0, v, (S0[s] + FILL[s]) % 2)
                            if i == 3:
                                split_max(s, slot, M0[s] + n + 2, v0 + v)
                            if i == 5:
                                v = copy_max(j, maxes_before(s, j) + 16 * NMAXD[s] * (g + 1), v0, v, (S0[s] + FILL[s]) % 2)
            for b in range(1, B):
                finish(STAGES - 1, b, 4 * (STAGES - 1) + b)

        @block.gpsimd
        def _(pool):
            def inverse_deviation(w, n):
                hold(pool, ln[w]["aggr"], NT * (n + 1))
                pool.tensor_scalar(rstd[:, 0], meanvar[:, :, 1], EPS, 1.0, ALU.add, ALU.mult).then_inc(ln[w]["eps"], 1)
                hold(pool, ln[w]["eps"], n + 1)
                pool.tensor_tensor(rstd[:, 1], rstd[:, 0], half_pow[:, :], ALU.pow).then_inc(ln[w]["rstd"], 1)

            def wide(row):
                return row.unsqueeze(1).to_broadcast([P, NT, C])

            def finish(s, b, kE):
                xb = x[:, b]
                pool.tensor_tensor(xb, xb, wide(bo[:, s]), ALU.add).then_inc(s_xb, 1)
                inverse_deviation("f", kE)
                if s < 2:
                    hold(pool, ln["f"]["xn"], NT * (kE + 1))
                    pool.tensor_tensor(xb, xb, wide(bff[:, :]), ALU.add).then_inc(s_fb, 1)

            def start(s, b, kP, par):
                inverse_deviation("a", kP)
                base = PL0[s] + b * POOLOPS[s]
                n = [0]

                def step(ins):
                    ins.then_inc(s_pl, 1)
                    n[0] += 1
                    hold(pool, s_pl, base + n[0])

                def split(src, dst, rest):
                    step(pool.tensor_copy(dst[:, 0], src))
                    step(pool.tensor_tensor(rest, src, dst[:, 0], ALU.subtract))
                    step(pool.tensor_copy(dst[:, 1], rest))
                    step(pool.tensor_tensor(dst[:, 2], rest, dst[:, 1], ALU.subtract))

                hold(pool, s_pe, G0[s] + b * GROUPS[s] + GROUPS[s] - (4 if s == RBF else 0))
                if not isinstance(kP, int) or kP > 0:
                    hold(pool, s_rec, 16 * (R0[s] + b * STORES[s]))
                K, Q, X, Y = (proj[:, i] for i in range(4))
                if s == RBF:
                    step(pool.tensor_tensor(work[:, 0], K, K, ALU.mult))
                    step(pool.tensor_tensor(work[:, 1], Q, Q, ALU.mult))
                if s == REL:
                    for i in range(2):
                        step(pool.tensor_tensor(work[:, 0], X, tables[:, 2 * i], ALU.mult))
                        step(pool.tensor_tensor(work[:, 1], Y, tables[:, 2 * i + 1], ALU.mult))
                        step(pool.tensor_tensor(work[:, 0], work[:, 0], work[:, 1], ALU.add))
                        split(work[:, 0], parts[:, 2 + i], work[:, 1])
                if s == ROPE:
                    hold(pool, s_tab, 32)
                    for z, zp in ((Q, X), (K, Y)):
                        step(pool.tensor_tensor(work[:, 0], z, tables[:, 0], ALU.mult))
                        step(pool.tensor_tensor(work[:, 1], zp, tables[:, 1], ALU.mult))
                        step(pool.tensor_tensor(z, work[:, 0], work[:, 1], ALU.add))
                rest = work if s != RBF else proj[:, 2:4]
                split(K, parts[:, 0], rest[:, 0])
                split(Q, parts[:, 1], rest[:, 1])
                if s == RBF:
                    hold(pool, s_pe, G0[s] + b * GROUPS[s] + GROUPS[s])
                    for m in range(2):
                        split(norms[:, m], nparts[:, m], norms[:, 2])
                if s != REL:
                    step(pool.tensor_tensor(values[:, par], values[:, par], wide(bv[:, s]), ALU.add))
                pool.memset(pool_flag[:, :], 0.0).then_inc(s_va, 1)
                assert n[0] == POOLOPS[s], (s, n[0])

            hold(pool, s_c, NCONST[0])
            hold(pool, s_dv, SETUP_DVE)
            hold(pool, s_x, 16 * B)
            start(0, 0, 0, 0)
            for s in range(STAGES):
                with pool.Fori(0, B) as b:
                    if s > 0:
                        with pool.If(b < B - 1):
                            finish(s - 1, (b + 1) % B, 4 * s + b - 3)
                    with pool.If(b == B - 1):
                        finish(s, 0, 4 * s)
                    with pool.If(b < B - 1):
                        start(s, (b + 1) % B, 4 * s + b + 1, (b + 1) % 2)
                    if s + 1 < STAGES:
                        with pool.If(b == B - 1):
                            start(s + 1, 0, 4 * s + 4, 0)
                    pool.nop()
            for b in range(1, B):
                finish(STAGES - 1, b, 4 * (STAGES - 1) + b)


def bf16_bits(v):
    u = np.ascontiguousarray(v, np.float32).view(np.uint32)
    return ((u + 0x7FFF + ((u >> 16) & 1)) >> 16).astype(np.uint16)


def bf16_parts(v):
    out, rest = [], np.array(v, np.float32)
    for _ in range(3):
        bits = bf16_bits(rest)
        out.append(bits)
        rest = rest - (bits.astype(np.uint32) << 16).view(np.float32)
    return out


def shape_constants():
    f = np.float32
    freq = f(1.0) / np.power(f(10000.0), np.arange(D // 2, dtype=f) / f(D // 2))
    pos = np.arange(2 * T, dtype=f)
    ang = (pos[:, None] * freq[None, :]).astype(np.float64)
    sin, cos = np.sin(ang).T, np.cos(ang).T
    own_sin = np.concatenate([sin, sin])
    swap_cos = np.concatenate([cos, -cos])

    def every_head(rows):
        return np.tile(rows, (H, 1)).astype(f)

    tables = np.stack([every_head(own_sin[:, :T]), every_head(swap_cos[:, :T]),
                       every_head(own_sin[:, T:]), every_head(swap_cos[:, T:]),
                       every_head(np.concatenate([cos, cos])[:, :T]), every_head(np.concatenate([-sin, sin])[:, :T])])
    key_parts = bf16_parts(np.concatenate([cos[:, :T], sin[:, :T]]).astype(f))
    def hide(where):
        return bf16_bits(np.where(where, f(BIG), f(0)))

    i = np.arange(P)
    wide = np.arange(P + 1)
    return {
        "tables": tables,
        "rel_rows": np.concatenate([key_parts[p] for p in KPARTS6]),
        "ones3": bf16_bits(np.ones((3, T), f)),
        "minus3": bf16_bits(-np.ones((3, T), f)),
        "rank": np.arange(NOPS, 0, -1).astype(f),
        "ident": np.eye(P, dtype=f),
        "ident_bf": bf16_bits(np.eye(P, dtype=f)),
        "hide_qk": hide(i[None, :] < i[:, None]),
        "hide_kq": hide(i[:, None] < i[None, :]),
        "low_qk": hide((wide[None, :] > i[:, None]) & ((wide[None, :] < P) | (i[:, None] == P - 1))),
        "low_kq": hide((wide[None, :] - 1 < i[:, None]) & ((wide[None, :] > 0) | (i[:, None] == 0))),
        "up_qk": hide(i[None, :] < i[:, None] + 2),
        "up_kq": hide(i[:, None] < i[None, :] + 2),
        "off_diag": hide(i[None, :] != i[:, None]),
        "neghalf": np.where(i[:, None] // D == np.arange(H)[None, :], f(-0.5), f(0)).astype(f),
    }


def swap_halves(v):
    w = v.reshape(*v.shape[:-1], -1, 2, D // 2)
    return np.ascontiguousarray(w[..., ::-1, :]).reshape(v.shape)


INPUTS = ["L0_attn_a_x", "L0_attn_a_Wqkv", "L0_attn_a_bqkv", "L0_attn_a_Wo", "L0_attn_a_bo", "L0_attn_b_Wqkv",
          "L0_attn_b_bqkv", "L0_attn_b_r_sigma", "L0_attn_b_Wproj", "L0_attn_b_bproj", "L0_ffn_W", "L0_ffn_b",
          "L0_ffn_logits", "L0_ffn_u", "L1_attn_a_Wq", "L1_attn_a_Wk", "L1_attn_a_Wv", "L1_attn_a_u", "L1_attn_a_v",
          "L1_attn_a_Wo", "L1_attn_a_bo", "L1_attn_b_Wq", "L1_attn_b_bq", "L1_attn_b_Wk", "L1_attn_b_bk",
          "L1_attn_b_Wv", "L1_attn_b_bv", "L1_attn_b_Wo", "L1_attn_b_bo"]


def kernel(**inputs):
    import concourse.bacc as bacc
    from concourse.bass_utils import run_bass_kernel_spmd

    nc = bacc.Bacc("TRN2", target_bir_lowering=False, num_devices=1)
    a = {n: np.ascontiguousarray(inputs[n]) for n in INPUTS}
    a["L0_attn_b_r_sigma"] = a["L0_attn_b_r_sigma"].reshape(1, 1)
    k = shape_constants()
    k["Wq_a_swapped"] = swap_halves(np.asarray(inputs["L1_attn_a_Wq"]))
    k["v_swapped"] = swap_halves(np.asarray(inputs["L1_attn_a_v"]))
    k["Wq_b_swapped"] = swap_halves(np.asarray(inputs["L1_attn_b_Wq"]))
    k["Wk_b_swapped"] = swap_halves(np.asarray(inputs["L1_attn_b_Wk"]))
    k["bq_swapped"] = swap_halves(np.asarray(inputs["L1_attn_b_bq"]))
    k["bk_swapped"] = swap_halves(np.asarray(inputs["L1_attn_b_bk"]))
    k["ffn_weight_T"] = np.ascontiguousarray(np.asarray(inputs["L1_ffn_weight"]).T)
    disha = np.asarray(inputs["L1_ffn_disha"])
    k["disha_twice"] = np.concatenate([disha, disha])
    arrays, aps = {}, {}
    for n, v in {**a, **k}.items():
        arrays[f"in_{n}"] = v
        aps[n] = nc.dram_tensor(f"in_{n}", v.shape, mybir.dt.from_np(v.dtype), kind="ExternalInput").ap()
    out = nc.dram_tensor("out_x", (B, T, C), F32, kind="ExternalOutput").ap()
    build(nc, aps, aps, out)
    r = run_bass_kernel_spmd(nc, [arrays], core_ids=[0])
    return r.results[0]["out_x"]
```
